# Optimizing a Trainium2 kernel written in Bass

```python
import numpy as np
import jax
import jax.numpy as jnp

def _softmax(x, axis=-1):
    return jax.nn.softmax(x, axis=axis)

def _gelu(x):
    return jax.nn.gelu(x, approximate=True)

def _silu(x):
    return jax.nn.silu(x)

def _sigmoid(x):
    return jax.nn.sigmoid(x)

def _layernorm(x, axis=-1, eps=1e-05):
    m = jnp.mean(x, axis=axis, keepdims=True)
    v = jnp.var(x, axis=axis, keepdims=True)
    return (x - m) / jnp.sqrt(v + eps)

def _scatter_add(tgt, idx, src, axis=0):
    return tgt.at[idx].add(src)

def _segment_sum(src, seg, n):
    return jax.ops.segment_sum(src, seg, n)
kernel_name = 'mk_early_fusion_d1_tok_img768_r4_19c204'

def setup_inputs(seed: int=0):
    np.random.seed(seed)
    _w = jnp.asarray

    def _rec_inputs():
        import jax
        import jax.numpy as jnp
        _rk = jax.random.key(seed)
        x = -0.000222058 + 0.999998 * jax.random.normal(jax.random.fold_in(_rk, 1), (16, 3, 96, 96), jnp.float32)
        txt = 0.00118357 + 0.999382 * jax.random.normal(jax.random.fold_in(_rk, 2), (16, 77, 192), jnp.float32)
        return (x, txt)
    x, txt = _rec_inputs()

    def _L0_tok_setup():
        import jax, jax.numpy as jnp
        import numpy as np
        B, C, H, W = (32, 3, 128, 128)
        PH, PW = (16, 16)
        EMBED = 192
        PATCH_DIM = C * PH * PW
        key = jax.random.key(seed)
        k1, k2, k3 = jax.random.split(key, 3)
        x = jax.random.normal(k1, (B, C, H, W), dtype=jnp.float32)
        proj_w = jax.random.normal(k2, (EMBED, PATCH_DIM), dtype=jnp.float32) * PATCH_DIM ** (-0.5)
        proj_b = jax.random.normal(k3, (EMBED,), dtype=jnp.float32) * 0.01
        return {'x': x, 'proj_w': proj_w, 'proj_b': proj_b}
    _L0_tok_all = _L0_tok_setup()
    _L0_tok_in = {k: v for k, v in _L0_tok_all.items() if k in ('proj_w', 'proj_b')}
    del _L0_tok_all

    def _L0_attn_setup():
        import jax, jax.numpy as jnp
        import numpy as np
        B, N, C = (32, 577, 192)
        H = 12
        D = C // H
        key = jax.random.key(seed)
        ks = jax.random.split(key, 4)
        x = jax.random.normal(ks[0], (B, N, C), dtype=jnp.float32)
        w_qkv = jax.random.normal(ks[1], (C, 3 * C), dtype=jnp.float32) * C ** (-0.5)
        b_qkv = jnp.zeros((3 * C,), dtype=jnp.float32)
        scale = jnp.ones((H,), dtype=jnp.float32) * D ** (-0.5)
        w_proj = jax.random.normal(ks[2], (C, C), dtype=jnp.float32) * C ** (-0.5)
        b_proj = jnp.zeros((C,), dtype=jnp.float32)
        return {'x': x, 'w_qkv': w_qkv, 'b_qkv': b_qkv, 'scale': scale, 'w_proj': w_proj, 'b_proj': b_proj}
    _L0_attn_all = _L0_attn_setup()
    _L0_attn_in = {k: v for k, v in _L0_attn_all.items() if k in ('w_qkv', 'b_qkv', 'scale', 'w_proj', 'b_proj')}
    del _L0_attn_all

    def _L0_ffn_setup():
        import jax, jax.numpy as jnp
        import numpy as np
        E = 16
        D = 192
        K = D // 2
        SI = 2 * D
        B, N = (8, 1024)

        def _moe_mlp(x, gw, uw, dw):
            return jax.nn.silu(x @ gw) * (x @ uw) @ dw
        key = jax.random.key(seed)
        ks = jax.random.split(key, 20)
        s = lambda fan_in: 1.0 / np.sqrt(fan_in)
        inp = {}
        inp['hidden_states'] = jax.random.normal(ks[0], (B, N, D), jnp.float32)
        inp['posembed'] = jax.random.normal(ks[1], (E, D), jnp.float32)
        inp['pos_w'] = jax.random.uniform(ks[2], (D, D), jnp.float32, -s(D), s(D))
        inp['pos_b'] = jax.random.uniform(ks[3], (D,), jnp.float32, -s(D), s(D))
        inp['gate_w'] = jax.random.uniform(ks[4], (D, D), jnp.float32, -s(D), s(D))
        inp['gate_b'] = jax.random.uniform(ks[5], (D,), jnp.float32, -s(D), s(D))
        inp['eg_w'] = jax.random.uniform(ks[6], (E, K, D), jnp.float32, -s(K), s(K))
        inp['eu_w'] = jax.random.uniform(ks[7], (E, K, D), jnp.float32, -s(K), s(K))
        inp['ed_w'] = jax.random.uniform(ks[8], (E, D, D), jnp.float32, -s(D), s(D))
        inp['sg_w'] = jax.random.uniform(ks[9], (D, SI), jnp.float32, -s(D), s(D))
        inp['su_w'] = jax.random.uniform(ks[10], (D, SI), jnp.float32, -s(D), s(D))
        inp['sd_w'] = jax.random.uniform(ks[11], (SI, D), jnp.float32, -s(SI), s(SI))
        inp['ln_g'] = jnp.ones((D,), jnp.float32)
        inp['ln_b'] = jnp.zeros((D,), jnp.float32)
        inp['m1_w'] = jax.random.uniform(ks[12], (D, D), jnp.float32, -s(D), s(D))
        inp['m1_b'] = jax.random.uniform(ks[13], (D,), jnp.float32, -s(D), s(D))
        inp['m2_w'] = jax.random.uniform(ks[14], (D, D), jnp.float32, -s(D), s(D))
        inp['m2_b'] = jax.random.uniform(ks[15], (D,), jnp.float32, -s(D), s(D))
        return inp
    _L0_ffn_all = _L0_ffn_setup()
    _L0_ffn_in = {k: v for k, v in _L0_ffn_all.items() if k in ('posembed', 'pos_w', 'pos_b', 'gate_w', 'gate_b', 'eg_w', 'eu_w', 'ed_w', 'sg_w', 'su_w', 'sd_w', 'ln_g', 'ln_b', 'm1_w', 'm1_b', 'm2_w', 'm2_b')}
    del _L0_ffn_all
    return {'x': x, 'txt': txt, 'L0_tok_proj_w': _L0_tok_in['proj_w'], 'L0_tok_proj_b': _L0_tok_in['proj_b'], 'L0_attn_w_qkv': _L0_attn_in['w_qkv'], 'L0_attn_b_qkv': _L0_attn_in['b_qkv'], 'L0_attn_scale': _L0_attn_in['scale'], 'L0_attn_w_proj': _L0_attn_in['w_proj'], 'L0_attn_b_proj': _L0_attn_in['b_proj'], 'L0_ffn_posembed': _L0_ffn_in['posembed'], 'L0_ffn_pos_w': _L0_ffn_in['pos_w'], 'L0_ffn_pos_b': _L0_ffn_in['pos_b'], 'L0_ffn_gate_w': _L0_ffn_in['gate_w'], 'L0_ffn_gate_b': _L0_ffn_in['gate_b'], 'L0_ffn_eg_w': _L0_ffn_in['eg_w'], 'L0_ffn_eu_w': _L0_ffn_in['eu_w'], 'L0_ffn_ed_w': _L0_ffn_in['ed_w'], 'L0_ffn_sg_w': _L0_ffn_in['sg_w'], 'L0_ffn_su_w': _L0_ffn_in['su_w'], 'L0_ffn_sd_w': _L0_ffn_in['sd_w'], 'L0_ffn_ln_g': _L0_ffn_in['ln_g'], 'L0_ffn_ln_b': _L0_ffn_in['ln_b'], 'L0_ffn_m1_w': _L0_ffn_in['m1_w'], 'L0_ffn_m1_b': _L0_ffn_in['m1_b'], 'L0_ffn_m2_w': _L0_ffn_in['m2_w'], 'L0_ffn_m2_b': _L0_ffn_in['m2_b']}

def reference(x, txt, L0_tok_proj_w, L0_tok_proj_b, L0_attn_w_qkv, L0_attn_b_qkv, L0_attn_scale, L0_attn_w_proj, L0_attn_b_proj, L0_ffn_posembed, L0_ffn_pos_w, L0_ffn_pos_b, L0_ffn_gate_w, L0_ffn_gate_b, L0_ffn_eg_w, L0_ffn_eu_w, L0_ffn_ed_w, L0_ffn_sg_w, L0_ffn_su_w, L0_ffn_sd_w, L0_ffn_ln_g, L0_ffn_ln_b, L0_ffn_m1_w, L0_ffn_m1_b, L0_ffn_m2_w, L0_ffn_m2_b):
    import jax
    import jax.numpy as jnp

    def _L0_tok_ref(x, proj_w, proj_b):
        import jax, jax.numpy as jnp
        import numpy as np
        B, C, H, W = (32, 3, 128, 128)
        PH, PW = (16, 16)
        EMBED = 192
        PATCH_DIM = C * PH * PW
        b, c, h, w = x.shape
        nh, nw = (h // PH, w // PW)
        patches = x.reshape(b, c, nh, PH, nw, PW)
        patches = patches.transpose(0, 2, 4, 1, 3, 5).reshape(b, nh * nw, c * PH * PW)
        out = jnp.einsum('blp,ep->ble', patches, proj_w) + proj_b
        return out

    def _L0_attn_ref(x, w_qkv, b_qkv, scale, w_proj, b_proj):
        import jax, jax.numpy as jnp
        import numpy as np
        B, N, C = (32, 577, 192)
        H = 12
        D = C // H
        b, n, c = x.shape
        h = scale.shape[0]
        d = c // h
        qkv = (x @ w_qkv + b_qkv).reshape(b, n, 3, h, d)
        q = qkv[:, :, 0]
        k = qkv[:, :, 1]
        v = qkv[:, :, 2]
        attn = jnp.einsum('bihd,bjhd->bhij', q, k) * scale[None, :, None, None]
        if n > 1:
            mask = jnp.zeros((n, n), dtype=bool).at[1:, 1:].set(jnp.eye(n - 1, dtype=bool))
            attn = jnp.where(mask[None, None], -jnp.inf, attn)
        attn = jax.nn.softmax(attn, axis=-1)
        out = jnp.einsum('bhij,bjhd->bihd', attn, v).reshape(b, n, c)
        return out @ w_proj + b_proj

    def _L0_ffn_ref(hidden_states, posembed, pos_w, pos_b, gate_w, gate_b, eg_w, eu_w, ed_w, sg_w, su_w, sd_w, ln_g, ln_b, m1_w, m1_b, m2_w, m2_b):
        import jax, jax.numpy as jnp
        import numpy as np
        E = 16
        D = 192
        K = D // 2
        SI = 2 * D
        B, N = (8, 1024)

        def _moe_mlp(x, gw, uw, dw):
            return jax.nn.silu(x @ gw) * (x @ uw) @ dw
        pe = jax.nn.softmax(posembed @ pos_w + pos_b, axis=-1)
        y = _moe_mlp(hidden_states, sg_w, su_w, sd_w)
        for i in range(E):
            gate_feature = hidden_states * pe[i] @ gate_w + gate_b
            gate_weight, gate_idx = jax.lax.top_k(gate_feature, K)
            gate_weight = jax.nn.softmax(gate_weight, axis=-1)
            gathered = jnp.take_along_axis(hidden_states, gate_idx, axis=-1)
            y = y + _moe_mlp(gathered * gate_weight, eg_w[i], eu_w[i], ed_w[i])
        mu = jnp.mean(y, axis=-1, keepdims=True)
        var = jnp.mean(jnp.square(y - mu), axis=-1, keepdims=True)
        yn = (y - mu) * jax.lax.rsqrt(var + 1e-06) * ln_g + ln_b
        return jax.nn.silu(yn @ m1_w + m1_b) @ m2_w + m2_b
    h = _L0_tok_ref(x, L0_tok_proj_w, L0_tok_proj_b)
    h = jnp.concatenate([h, txt], axis=1)
    h = h + _L0_attn_ref(_layernorm(h, axis=-1), L0_attn_w_qkv, L0_attn_b_qkv, L0_attn_scale, L0_attn_w_proj, L0_attn_b_proj)
    h = h + _L0_ffn_ref(_layernorm(h, axis=-1), L0_ffn_posembed, L0_ffn_pos_w, L0_ffn_pos_b, L0_ffn_gate_w, L0_ffn_gate_b, L0_ffn_eg_w, L0_ffn_eu_w, L0_ffn_ed_w, L0_ffn_sg_w, L0_ffn_su_w, L0_ffn_sd_w, L0_ffn_ln_g, L0_ffn_ln_b, L0_ffn_m1_w, L0_ffn_m1_b, L0_ffn_m2_w, L0_ffn_m2_b)
    return h

_drawn_inputs = setup_inputs


def setup_inputs(seed=0):
    import zlib

    import numpy as np

    out = dict(_drawn_inputs(seed))
    spreads = {'L0_attn_b_qkv': (0.0, 0.1),
     'L0_attn_scale': (0.25, 0.2),
     'L0_attn_b_proj': (0.0, 0.1),
     'L0_ffn_ln_g': (1.0, 0.2),
     'L0_ffn_ln_b': (0.0, 0.449)}
    factors = {'L0_tok_proj_b': 8.0,
     'L0_ffn_posembed': 8.0,
     'L0_ffn_pos_w': 8.0,
     'L0_ffn_pos_b': 22.76,
     'L0_ffn_gate_w': 8.0,
     'L0_ffn_gate_b': 8.0,
     'L0_ffn_eg_w': 8.0,
     'L0_ffn_eu_w': 8.0,
     'L0_ffn_ed_w': 8.0,
     'L0_ffn_m1_b': 4.347}
    for name, (base, spread) in spreads.items():
        noise = np.random.default_rng([zlib.crc32(name.encode()), seed]).standard_normal(out[name].shape)
        drawn = base * np.exp(spread * noise) if base else spread * noise
        out[name] = jnp.asarray(drawn.astype(out[name].dtype))
    for name, factor in factors.items():
        out[name] = (out[name] * factor).astype(out[name].dtype)
    return out
```

```python
from contextlib import ExitStack

import concourse.bass as bass
from concourse import mybir

F32 = mybir.dt.float32
BF16 = mybir.dt.bfloat16
U16 = mybir.dt.uint16
U8 = mybir.dt.uint8
ALU = mybir.AluOpType
ACT = mybir.ActivationFunctionType
AX_X = mybir.AxisListType.X

IMAGES, CHANNELS, SIDE, PATCH = 16, 3, 96, 16
PATCHES = (SIDE // PATCH) ** 2
TEXT = 77
TOK = PATCHES + TEXT
TOKENS = IMAGES * TOK
PDIM = CHANNELS * PATCH * PATCH
PCH = PDIM // 128
D = 192
HALF = D // 2
HEADS, DH = 12, 16
HG = HEADS // 4
EXPERTS = 16
TOP = D // 2
ROUNDS = TOP // 8
SHARED = 2 * D
GRP = 4
BPT = EXPERTS // GRP
COLS = GRP * TOP
TILE = 128
OCT = 16
PER = TILE // OCT
LO, HI = 16, D // 16
STEP = 120
TILES = (TOKENS - TILE) // STEP + 1
assert (TILES - 1) * STEP + TILE == TOKENS
QO = 4
PIECES = OCT // QO
UNITS = EXPERTS + SHARED // D
NEG = -3.0e38
MASKED = -1.0e30
EPS1, EPS2 = 1e-5, 1e-6


def build(nc, patches, txt, w_patch, b_patch, w_qk, scale, w_v, w_o, pos_t, w_pos, w_gate, b_gate, w_shared,
          w_sdown, w_exp, w_down, w_m1, w_m2, cols, ident_in, place_in, own_in, mask_in, out):
    tok_d = nc.dram_tensor("tok_d", [TOKENS, D], F32, kind="Internal").ap()
    norm_d = nc.dram_tensor("norm_d", [TOKENS, D], F32, kind="Internal").ap()
    normt_d = nc.dram_tensor("normt_d", [HALF, 2, TOKENS], F32, kind="Internal").ap()
    idx_d = nc.dram_tensor("idx_d", [2, 2, TILE, COLS], U8, kind="Internal").ap()

    with ExitStack() as ctx:
        def sb(name, shape, dt=F32):
            return ctx.enter_context(nc.sbuf_tensor(name, shape, dt))

        def sem(name):
            return ctx.enter_context(nc.semaphore(name))

        ident = sb("ident", [128, 128])
        wgate = sb("wgate", [HALF + 1, 2, EXPERTS, D])
        wshared = sb("wshared", [HALF, 2, 4, D])
        wsdown = sb("wsdown", [HALF, 4, D])
        wexp = sb("wexp", [TOP, EXPERTS, 2 * D])
        wdown = sb("wdown", [HALF, EXPERTS, 2, D])
        wm1 = sb("wm1", [HALF, 2, D])
        wm2 = sb("wm2", [HALF + 1, 2, D])
        colv = sb("colv", [HALF, 8])
        place = sb("place", [128, 16 + 128])
        own = sb("own", [HALF, PER])
        lowv = sb("lowv", [128, 4])
        ps = ctx.enter_context(nc.psum_tensor("ps", [128, 8, 512], F32))

        consts_in = sem("consts_in")
        stored = sem("stored")
        consts = [(ident, ident_in), (wshared, w_shared), (wsdown, w_sdown), (wexp, w_exp), (wdown, w_down),
                  (wm1, w_m1), (wm2, w_m2), (colv, cols[0:HALF, 0:8]), (place, place_in), (own, own_in),
                  (lowv, cols[:, 8:12])]
        CONSTS = 16 * len(consts)

        attention(nc, patches, txt, w_patch, b_patch, w_qk, scale, w_v, w_o, pos_t, w_pos, w_gate, b_gate, mask_in,
                  tok_d, norm_d, normt_d, ident, wgate, lowv, ps, consts, consts_in, CONSTS, stored)
        experts(nc, sb, sem, tok_d, norm_d, normt_d, idx_d, out, ident, wgate, wshared, wsdown, wexp, wdown,
                wm1, wm2, colv, place, own, lowv, ps, consts_in, CONSTS)


def attention(nc, patches, txt, w_patch, b_patch, w_qk, scale, w_v, w_o, pos_t, w_pos, w_gate, b_gate, mask_in,
              tok_d, norm_d, normt_d, ident, wgate, lowv, ps, consts, consts_in, CONSTS, stored):
    with ExitStack() as ctx:
        def sb(name, shape, dt=F32):
            return ctx.enter_context(nc.sbuf_tensor(name, shape, dt))

        def sem(name):
            return ctx.enter_context(nc.semaphore(name))

        wpatch = sb("wpatch", [128, PCH, D])
        bpatch = sb("bpatch", [1, D])
        wqk = sb("wqk", [HALF + 1, 2, 2 * HG, 128])
        scl = sb("scl", [HALF + 1, HG, 4])
        wv = sb("wv", [HALF + 1, 2, D])
        wo = sb("wo", [HALF + 1, 2, D])
        post = sb("post", [HALF + 1, 2, EXPERTS])
        wpos = sb("wpos", [HALF + 1, 2, D])
        gatew = sb("gatew", [HALF, 2, D])
        pe_row = sb("pe_row", [EXPERTS, D])
        pe_col = sb("pe_col", [HALF, 2, EXPERTS])
        pstat = sb("pstat", [EXPERTS, 4])
        mask = sb("mask", [TOK, 4, TOK])
        maskb = sb("maskb", [TOK, 4, TOK], BF16)
        identb = sb("identb", [128, 128], BF16)
        ones = sb("ones", [1, 128])
        patch = sb("patch", [128, PCH, PATCHES])
        h = sb("h", [TOK, D])
        xn = sb("xn", [TOK, D])
        xt = sb("xt", [HALF + 1, 2, TOK])
        qt = sb("qt", [128, HG, TOK])
        kz = sb("kz", [128, HG, 4, TOK])
        v = sb("v", [TOK, D])
        prob = sb("prob", [TOK, HEADS, TOK])
        probt = sb("probt", [TOK, HEADS, TOK])
        o = sb("o", [TOK, D])
        ot = sb("ot", [HALF + 1, 2, TOK])
        h2 = sb("h2", [TOK, D])
        hs = sb("hs", [TOK, D])
        hst = sb("hst", [HALF, 2, TOK])
        bst = sb("bst", [TOK, 6])
        mv = sb("mv", [TOK, 2])
        bst2 = sb("bst2", [TOK, 6])
        mv2 = sb("mv2", [TOK, 2])
        ve = sb("ve", [TOK, 2])
        rstd = sb("rstd", [TOK, 2])
        nmax = sb("nmax", [TOK, HEADS])
        rsum = sb("rsum", [TOK, HEADS])
        rinv = sb("rinv", [TOK, HEADS])

        early_in = sem("early_in")
        zeroed = sem("zeroed")
        setup_pe = sem("setup_pe")
        setup_vec = sem("setup_vec")
        setup_act = sem("setup_act")
        patch_in = sem("patch_in")
        text_in = sem("text_in")
        embedded = sem("embedded")
        tokens_ready = sem("tokens_ready")
        stats1 = sem("stats1")
        var1 = sem("var1")
        ve1 = sem("ve1")
        rstd1 = sem("rstd1")
        normed = sem("normed")
        transposed = sem("transposed")
        xt_ready = sem("xt_ready")
        qkv_done = sem("qkv_done")
        q_ready = sem("q_ready")
        k_ready = sem("k_ready")
        v_ready = sem("v_ready")
        scored = sem("scored")
        max_ready = sem("max_ready")
        probs = sem("probs")
        probs_turned = sem("probs_turned")
        turned_act = sem("turned_act")
        turned_vec = sem("turned_vec")
        mixed = sem("mixed")
        rinv_ready = sem("rinv_ready")
        o_ready = sem("o_ready")
        ot_ready = sem("ot_ready")
        projected = sem("projected")
        h2_ready = sem("h2_ready")
        stats2 = sem("stats2")
        var2 = sem("var2")
        ve2 = sem("ve2")
        rstd2 = sem("rstd2")
        hs_ready = sem("hs_ready")
        hst_ready = sem("hst_ready")
        tok_out = sem("tok_out")
        norm_out = sem("norm_out")
        normt_out = sem("normt_out")

        early = [(wpatch, w_patch), (bpatch, b_patch), (wqk, w_qk), (scl, scale), (wv, w_v), (wo, w_o),
                 (post, pos_t), (wpos, w_pos), (gatew, w_gate), (mask, mask_in),
                 (wgate, b_gate)]
        EARLY = 16 * (len(early))

        passed = sem("passed")

        def steady(eng):
            eng.sem_inc(passed, 1)

        block = ctx.enter_context(nc.Block())

        @block.sync
        def _(sp):
            for dst, src in early:
                if dst is scl:
                    sp.dma_start(scl[:], bass.AP(tensor=scale.tensor, offset=0, ap=[[0, HALF + 1], [4, HG], [1, 4]])).then_inc(early_in, 16)
                elif dst is wgate:
                    sp.dma_start(wgate[HALF:HALF + 1, 1, :, :],
                                 bass.AP(tensor=b_gate.tensor, offset=0, ap=[[0, 1], [0, EXPERTS], [1, D]])).then_inc(early_in, 16)
                else:
                    sp.dma_start(dst[:], src).then_inc(early_in, 16)
            for dst, src in consts:
                sp.dma_start(dst[:], src).then_inc(consts_in, 16)
            with sp.Fori(0, IMAGES) as i:
                sp.wait_ge(embedded, i)
                sp.dma_start(patch[:], patches[i]).then_inc(patch_in, 16)
                sp.wait_ge(h2_ready, i)
                sp.dma_start(h[PATCHES:TOK, :], txt[i]).then_inc(text_in, 16)
                sp.wait_ge(h2_ready, i + 1)
                sp.dma_start(tok_d[bass.ds(i * TOK, TOK), :], h2[:]).then_inc(tok_out, 16)
                sp.wait_ge(hs_ready, i + 1)
                sp.dma_start(norm_d[bass.ds(i * TOK, TOK), :], hs[:]).then_inc(norm_out, 16)
                sp.wait_ge(hst_ready, i + 1)
                steady(sp)
                sp.dma_start(normt_d[:, :, bass.ds(i * TOK, TOK)], hst[:]).then_inc(normt_out, 16)
            sp.wait_ge(tok_out, 16 * IMAGES)
            sp.wait_ge(norm_out, 16 * IMAGES)
            sp.wait_ge(normt_out, 16 * IMAGES)

        @block.gpsimd
        def _(pool):
            nc.gpsimd.memset(kz[:], 0.0).then_inc(zeroed, 1)
            pool.wait_ge(consts_in, CONSTS)
            with pool.Fori(0, IMAGES) as i:
                for n, (var, ready, done, eps, m) in enumerate(((var1, ve1, rstd1, EPS1, mv), (var2, ve2, rstd2, EPS1, mv2))):
                    pool.wait_ge(var, i + 1)
                    steady(pool)
                    nc.gpsimd.tensor_scalar(ve[:, n:n + 1], m[:, 1:2], 1.0, eps, ALU.mult, ALU.add).then_inc(ready, 1)
                    pool.wait_ge(ready, i + 1)
                    nc.gpsimd.tensor_tensor(rstd[:, n:n + 1], ve[:, n:n + 1], lowv[0:TOK, 1:2], ALU.pow).then_inc(done, 1)

        @block.scalar
        def _(act):
            act.wait_ge(early_in, EARLY)
            nc.scalar.activation(maskb[:], mask[:], ACT.Copy).then_inc(setup_act, 1)
            act.wait_ge(consts_in, CONSTS)
            nc.scalar.activation(identb[:], ident[:], ACT.Copy).then_inc(setup_act, 1)
            act.wait_ge(setup_vec, 2)
            nc.scalar.activation(pe_row[:], ps[0:EXPERTS, 0, 0:D], ACT.Exp, bias=pstat[:, 0:1],
                                 accum_out=pstat[:, 1:2]).then_inc(setup_act, 1)
            act.wait_ge(setup_pe, 2)
            nc.scalar.activation(pe_col[:], ps[0:HALF, 1, 0:2 * EXPERTS].rearrange("p (c e) -> p c e", c=2),
                                 ACT.Copy).then_inc(setup_act, 1)
            with act.Fori(0, IMAGES) as i:
                act.wait_ge(embedded, i + 1)
                act.wait_ge(h2_ready, i)
                nc.scalar.activation(h[0:PATCHES, :], ps[0:PATCHES, 0, 0:D], ACT.Copy).then_inc(tokens_ready, 1)
                act.wait_ge(transposed, 3 * i + 1)
                nc.scalar.activation(xt[0:HALF, :, :], turn_view(ps), ACT.Copy).then_inc(xt_ready, 1)
                act.wait_ge(qkv_done, 3 * i + 2)
                for j in range(2):
                    nc.scalar.activation(kz[32 * j:32 * j + 32, :, j, :], heads_view(ps[32 * j:32 * j + 32, 3, 0:HG * TOK]),
                                         ACT.Copy).then_inc(k_ready, 1)
                act.wait_ge(qkv_done, 3 * i + 3)
                nc.scalar.activation(v[:], ps[0:TOK, 4, 0:D], ACT.Copy).then_inc(v_ready, 1)
                act.wait_ge(max_ready, i + 1)
                for hd in range(HEADS):
                    ins = nc.scalar.activation(prob[:, hd, :], ps[0:TOK, 5 + hd // 4, (hd % 4) * TOK:(hd % 4 + 1) * TOK],
                                               ACT.Exp, bias=nmax[:, hd:hd + 1], accum_out=rsum[:, hd:hd + 1])
                    if hd % 4 == 3:
                        ins.then_inc(probs, 1)
                for c in (0, 2):
                    act.wait_ge(probs_turned, 3 * i + c + 1)
                    nc.scalar.activation(probt[:, 4 * c:4 * c + 4, :], quad_view(ps, 2 + c), ACT.Copy).then_inc(turned_act, 1)
                act.wait_ge(transposed, 3 * i + 2)
                nc.scalar.activation(ot[0:HALF, :, :], turn_view(ps), ACT.Copy).then_inc(ot_ready, 1)
                act.wait_ge(transposed, 3 * i + 3)
                act.wait_ge(normt_out, 16 * i)
                nc.scalar.activation(hst[:], turn_view(ps), ACT.Copy).then_inc(hst_ready, 1)

        @block.vector
        def _(dve):
            nc.vector.memset(xt[HALF:HALF + 1, :, :], 1.0).then_inc(zeroed, 1)
            nc.vector.memset(ot[HALF:HALF + 1, :, :], 1.0).then_inc(zeroed, 1)
            nc.vector.memset(ones[:], 1.0).then_inc(zeroed, 1)
            dve.wait_ge(early_in, EARLY)
            nc.vector.tensor_tensor(
                wqk[:, :, 0:HG, :].rearrange("p k c (h d) -> p k (c h) d", h=4),
                wqk[:, :, 0:HG, :].rearrange("p k c (h d) -> p k (c h) d", h=4),
                bass.AP(tensor=scl[:].tensor, offset=scl[:].offset,
                        ap=[list(scl[:].ap[0]), [0, 2], [1, HEADS], [0, 32]]), ALU.mult).then_inc(setup_vec, 1)
            dve.wait_ge(setup_pe, 1)
            nc.vector.tensor_reduce(pstat[:, 0:1], ps[0:EXPERTS, 0, 0:D], AX_X, ALU.max, negate=True).then_inc(setup_vec, 1)
            dve.wait_ge(setup_act, 3)
            nc.vector.reciprocal(pstat[:, 2:3], pstat[:, 1:2]).then_inc(setup_vec, 1)
            dve.wait_ge(setup_vec, 3)
            nc.vector.tensor_scalar(pe_row[:], pe_row[:], pstat[:, 2:3], None, ALU.mult).then_inc(setup_vec, 1)
            dve.wait_ge(setup_act, 4)
            for e in range(EXPERTS):
                for k in range(2):
                    nc.vector.tensor_scalar(wgate[0:HALF, k, e, :], gatew[:, k, :], pe_col[:, k, e:e + 1], None,
                                            ALU.mult).then_inc(setup_vec, 1)
            with dve.Fori(0, IMAGES) as i:
                def norm(src, bstats, m, stats, var, done, n, dst, ready):
                    nc.vector.bn_stats(bstats[:], src[:]).then_inc(stats, 1)
                    dve.wait_ge(stats, i + 1)
                    steady(dve)
                    nc.vector.bn_aggr(m[:], bstats[:]).then_inc(var, 1)
                    dve.wait_ge(done, i + 1)
                    nc.vector.tensor_scalar(dst[:], src[:], m[:, 0:1], rstd[:, n:n + 1], ALU.subtract,
                                            ALU.mult).then_inc(ready, 1)

                dve.wait_ge(tokens_ready, i + 1)
                dve.wait_ge(text_in, 16 * i + 16)
                norm(h, bst, mv, stats1, var1, rstd1, 0, xn, normed)
                dve.wait_ge(qkv_done, 3 * i + 1)
                nc.vector.tensor_copy(qt[:], ps[:, 2, 0:HG * TOK].rearrange("p (c j) -> p c j", c=HG)).then_inc(q_ready, 1)
                dve.wait_ge(qkv_done, 3 * i + 2)
                for j in range(2, 4):
                    nc.vector.tensor_copy(kz[32 * j:32 * j + 32, :, j, :],
                                          heads_view(ps[32 * j:32 * j + 32, 3, 0:HG * TOK])).then_inc(k_ready, 1)
                dve.wait_ge(scored, i + 1)
                nc.vector.tensor_reduce(nmax[:], ps[0:TOK, 5:8, 0:4 * TOK].rearrange("p c (h j) -> p c h j", h=4),
                                        AX_X, ALU.max, negate=True).then_inc(max_ready, 1)
                dve.wait_ge(probs_turned, 3 * i + 2)
                nc.vector.tensor_copy(probt[:, 4:8, :], quad_view(ps, 3)).then_inc(turned_vec, 1)
                dve.wait_ge(probs, 3 * i + 3)
                nc.vector.reciprocal(rinv[:], rsum[:]).then_inc(rinv_ready, 1)
                dve.wait_ge(rinv_ready, i + 1)
                dve.wait_ge(mixed, i + 1)
                nc.vector.tensor_tensor(o[:].rearrange("p (h d) -> p h d", h=HEADS),
                                        ps[0:TOK, 0, 0:D].rearrange("p (h d) -> p h d", h=HEADS),
                                        bass.AP(tensor=rinv[:].tensor, offset=rinv[:].offset,
                                                ap=[list(rinv[:].ap[0]), [1, HEADS], [0, DH]]),
                                        ALU.mult).then_inc(o_ready, 1)
                dve.wait_ge(projected, i + 1)
                dve.wait_ge(tok_out, 16 * i)
                nc.vector.tensor_tensor(h2[:], ps[0:TOK, 0, 256:256 + D], h[:], ALU.add).then_inc(h2_ready, 1)
                dve.wait_ge(h2_ready, i + 1)
                dve.wait_ge(norm_out, 16 * i)
                norm(h2, bst2, mv2, stats2, var2, rstd2, 1, hs, hs_ready)

        @block.tensor
        def _(pe):
            pe.wait_ge(early_in, EARLY)
            for k in range(2):
                last = nc.tensor.matmul(ps[0:EXPERTS, 0, 0:D], post[0:HALF + k, k, :], wpos[0:HALF + k, k, :],
                                        start=(k == 0), stop=(k == 1))
            last.then_inc(setup_pe, 1)
            pe.wait_ge(consts_in, CONSTS)
            pe.wait_ge(setup_vec, 4)
            for k in range(2):
                last = nc.tensor.transpose(ps[0:HALF, 1, EXPERTS * k:EXPERTS * (k + 1)], pe_row[:, HALF * k:HALF * (k + 1)],
                                           ident[0:EXPERTS, 0:EXPERTS])
            last.then_inc(setup_pe, 1)
            pe.wait_ge(setup_act, 4)
            pe.wait_ge(zeroed, 4)
            with pe.Fori(0, IMAGES) as i:
                def turn(src):
                    for k in range(2):
                        last = nc.tensor.transpose(ps[0:HALF, 1, 128 * k:128 * k + TOK], src[:, HALF * k:HALF * (k + 1)],
                                                   ident[0:TOK, 0:TOK])
                    last.then_inc(transposed, 1)

                pe.wait_ge(patch_in, 16 * i + 16)
                pe.wait_ge(h2_ready, i)
                for c in range(PCH):
                    nc.tensor.matmul(ps[0:PATCHES, 0, 0:D], patch[:, c, :], wpatch[:, c, :], start=(c == 0), stop=False)
                nc.tensor.matmul(ps[0:PATCHES, 0, 0:D], ones[0:1, 0:PATCHES], bpatch[:], start=False,
                                 stop=True).then_inc(embedded, 1)
                pe.wait_ge(normed, i + 1)
                pe.wait_ge(hst_ready, i)
                turn(xn)
                pe.wait_ge(xt_ready, i + 1)
                for w in range(2):
                    for c in range(HG):
                        for k in range(2):
                            last = nc.tensor.matmul(ps[:, 2 + w, c * TOK:(c + 1) * TOK], wqk[0:HALF + k, k, HG * w + c, :],
                                                    xt[0:HALF + k, k, :], start=(k == 0), stop=(k == 1))
                    last.then_inc(qkv_done, 1)
                for k in range(2):
                    last = nc.tensor.matmul(ps[0:TOK, 4, 0:D], xt[0:HALF + k, k, :], wv[0:HALF + k, k, :],
                                            start=(k == 0), stop=(k == 1))
                last.then_inc(qkv_done, 1)
                for c in range(HG):
                    nc.tensor.matmul(ps[0:TOK, 5 + c, 0:4 * TOK], identb[0:TOK, 0:TOK], maskb[:], start=True, stop=False)
                pe.wait_ge(q_ready, i + 1)
                pe.wait_ge(k_ready, 4 * i + 4)
                for c in range(HG):
                    last = nc.tensor.matmul(ps[0:TOK, 5 + c, 0:4 * TOK], qt[:, c, :], kz[:, c, :, :], start=False, stop=True)
                last.then_inc(scored, 1)
                pe.wait_ge(v_ready, i + 1)
                for c in range(HG):
                    pe.wait_ge(probs, 3 * i + c + 1)
                    for j in range(4):
                        last = nc.tensor.transpose(ps[0:TOK, 2 + c, j * TOK:(j + 1) * TOK], prob[:, 4 * c + j, :],
                                                   ident[0:TOK, 0:TOK])
                    last.then_inc(probs_turned, 1)
                pe.wait_ge(turned_act, 2 * i + 2)
                pe.wait_ge(turned_vec, i + 1)
                for hd in range(HEADS):
                    last = nc.tensor.matmul(ps[0:TOK, 0, hd * DH:(hd + 1) * DH], probt[:, hd, :], v[:, hd * DH:(hd + 1) * DH],
                                            start=True, stop=True)
                last.then_inc(mixed, 1)
                pe.wait_ge(o_ready, i + 1)
                turn(o)
                pe.wait_ge(ot_ready, i + 1)
                for k in range(2):
                    last = nc.tensor.matmul(ps[0:TOK, 0, 256:256 + D], ot[0:HALF + k, k, :], wo[0:HALF + k, k, :],
                                            start=(k == 0), stop=(k == 1))
                last.then_inc(projected, 1)
                pe.wait_ge(hs_ready, i + 1)
                turn(hs)


def turn_view(ps):
    return ps[0:HALF, 1, 0:256].rearrange("p (k j) -> p k j", k=2)[:, :, 0:TOK]


def heads_view(bank):
    return bank.rearrange("p (c j) -> p c j", c=HG)


def quad_view(ps, bank):
    return ps[0:TOK, bank, 0:4 * TOK].rearrange("p (h j) -> p h j", h=4)


GATE_B, LOOK_B, XG_B, XT_B, GU_B, Y_B, FIN_B = 0, 1, 3, 4, 5, 6, 7


def units_of(m):
    first = [(0, None, 0), (1, None, 1)] if m == 0 else []
    return first + [(2 + GRP * m + j, GRP * m + j, None) for j in range(GRP)]


def unit_spots(m):
    n = len(units_of(m))
    return [4 + 3 * j for j in range(n)] if n == 4 else [3 + 2 * j for j in range(n)]


def experts(nc, sb, sem, tok_d, norm_d, normt_d, idx_d, out, ident, wgate, wshared, wsdown, wexp, wdown,
            wm1, wm2, colv, place, own, lowv, ps, consts_in, CONSTS):
    keys = sb("keys", [TILE, BPT, GRP, D])
    vals = sb("vals", [TILE, 2, GRP, TOP])
    idx = sb("idx", [TILE, 2, GRP, TOP], U16)
    digits = sb("digits", [TILE, 2, 2, COLS], U8)
    ntop = sb("ntop", [TILE, 2, GRP])
    esum = sb("esum", [TILE, 2, GRP])
    einv = sb("einv", [TILE, 2, GRP])
    ew = sb("ew", [TILE, 2, GRP, TOP])
    hi_b = sb("hi_b", [HALF, OCT, COLS], U8)
    lo_b = sb("lo_b", [TILE, OCT, COLS], U8)
    hot = sb("hot", [HALF, OCT, COLS], BF16)
    lomask = sb("lomask", [TILE, OCT, COLS], BF16)
    looked_s = sb("looked_s", [TILE, 4, COLS])
    picked = sb("picked", [TILE, 4, COLS])
    xs = sb("xs", [TILE, GRP, TOP])
    xw = sb("xw", [TILE, GRP, TOP])
    xwt = sb("xwt", [TOP, GRP, TILE])
    gate_s = sb("gate_s", [HALF, 2, 2, TILE])
    up_s = sb("up_s", [HALF, 2, 2, TILE])
    hid = sb("hid", [HALF, 2, 2, TILE])
    nt_gate = sb("nt_gate", [HALF + 1, 2, TILE])
    nt_mlp = sb("nt_mlp", [HALF, 2, TILE])
    hr = sb("hr", [HALF, OCT, LO])
    rest = sb("rest", [HALF, OCT, LO])
    parts = sb("parts", [HALF, 3, OCT, LO], BF16)
    table = sb("table", [HALF, 3, OCT, TILE], BF16)
    resid = sb("resid", [TILE, D])
    y = sb("y", [TILE, D])
    ysq = sb("ysq", [TILE, D])
    yn = sb("yn", [TILE, D])
    st = sb("st", [TILE, 6])
    zt = sb("zt", [HALF, 2, TILE])
    st1 = sb("st1", [HALF + 1, 2, TILE])
    m2s = sb("m2s", [TILE, D])
    fin = sb("fin", [TILE, D])

    nt_gate_in, nt_mlp_in, hr_in, resid_in = sem("nt_gate_in"), sem("nt_mlp_in"), sem("hr_in"), sem("resid_in")
    b_ones = sem("b_ones")
    gated, keys_ready = sem("gated"), sem("keys_ready")
    chain = sem("chain")
    ranked, digits_out = sem("ranked"), sem("digits_out")
    ranks_done = sem("ranks_done")
    inverted = sem("inverted")
    weights_ready = sem("weights_ready")
    hi_in = [sem(f"hi_in{q}") for q in range(PIECES)]
    lo_in = [sem(f"lo_in{q}") for q in range(PIECES)]
    distance, hot_ready, masked = sem("distance"), sem("hot_ready"), sem("masked")
    rounded = sem("rounded")
    split, table_ready = sem("split"), sem("table_ready")
    looked, looked_out, picked_ready, placed = sem("looked"), sem("looked_out"), sem("picked_ready"), sem("placed")
    scaled, weighted, x_turned, xwt_ready = sem("scaled"), sem("weighted"), sem("x_turned"), sem("xwt_ready")
    gate_up, activated, hidden, downed = sem("gate_up"), sem("activated"), sem("hidden"), sem("downed")
    y_out, mean_ready, squared, var_ready, rstd_ready = (sem("y_out"), sem("mean_ready"), sem("squared"),
                                                         sem("var_ready"), sem("rstd_ready"))
    shift_ready, yn_ready, y_turned, zt_ready = sem("shift_ready"), sem("yn_ready"), sem("y_turned"), sem("zt_ready")
    m1_done, st1_ready, m2_done, m2_out, fin_ready = (sem("m1_done"), sem("st1_ready"), sem("m2_done"),
                                                      sem("m2_out"), sem("fin_ready"))
    out_done = sem("out_done")

    passed = sem("passed")

    def steady(eng):
        eng.sem_inc(passed, 1)

    def slots(eng, slot):
        slot(0, 0, False)
        with eng.Fori(0, TILES - 1) as t:
            for g in range(1, BPT):
                slot(t, g, True)
            slot(t + 1, 0, True)
        for g in range(1, BPT):
            slot(TILES - 1, g, True)

    def last_tile(t):
        return isinstance(t, int) and t == TILES - 1

    with nc.Block() as block:

        @block.sync
        def _(sp):
            def load_gate(t):
                sp.dma_start(nt_gate[0:HALF, :, :], normt_d[:, :, bass.ds(t * STEP, TILE)]).then_inc(nt_gate_in, 16)
                for j in range(PER):
                    src = norm_d[bass.ds(t * STEP + j * OCT, OCT), :].rearrange("o (hi lo) -> hi o lo", lo=LO)
                    sp.dma_start(hr[HI * j:HI * (j + 1), :, :], src).then_inc(hr_in, 16)

            def load_mlp(t):
                sp.dma_start(nt_mlp[:], normt_d[:, :, bass.ds(t * STEP, TILE)]).then_inc(nt_mlp_in, 16)

            load_gate(0)
            load_mlp(0)

            def slot(t, g, mlp):
                n, par = t * BPT + g, g % 2
                sp.wait_ge(ranked, n + 1)
                sp.dma_start(idx_d[par].rearrange("a p c -> p a c"), digits[:, par]).then_inc(digits_out, 16)
                sp.wait_ge(digits_out, 16 * n + 16)
                steady(sp)
                if mlp:
                    sp.wait_ge(hot_ready, PIECES * n)
                    sp.wait_ge(masked, PIECES * n)
                steady(sp)
                for q in range(PIECES):
                    for a, rows, dst, arrived in ((1, HI, hi_b, hi_in), (0, LO, lo_b, lo_in)):
                        base = idx_d[par, a, :, :]
                        src = bass.AP(tensor=base.tensor, offset=base.offset + q * QO * COLS,
                                      ap=[[OCT * COLS, PER], [0, rows], [1, QO * COLS]])
                        sp.dma_start(dst[:, q * QO:(q + 1) * QO, :], src).then_inc(arrived[q], 16)
                if g == 1 and not last_tile(t):
                    sp.wait_ge(gated, 2 * BPT * t + 2 * BPT)
                    steady(sp)
                    sp.wait_ge(split, t + 1)
                    steady(sp)
                    load_gate(t + 1)
                if g == 2:
                    sp.wait_ge(fin_ready, t)
                    sp.dma_start(resid[:], tok_d[bass.ds(t * STEP, TILE), :]).then_inc(resid_in, 16)
                    if not last_tile(t):
                        sp.wait_ge(gate_up, UNITS * t + 2)
                        load_mlp(t + 1)

            slots(sp, slot)
            sp.wait_ge(out_done, 16 * TILES)

        @block.vector
        def _(dve):
            nc.vector.memset(nt_gate[HALF:HALF + 1, :, :], 1.0).then_inc(b_ones, 1)
            nc.vector.memset(st1[HALF:HALF + 1, :, :], 1.0).then_inc(b_ones, 1)

            def invert(n, par):
                dve.wait_ge(weights_ready, n + 1)
                nc.vector.reciprocal(einv[:, par, :], esum[:, par, :]).then_inc(inverted, 1)

            def slot(t, g, mlp):
                n, par = t * BPT + g, g % 2
                for pair in range(2):
                    dve.wait_ge(keys_ready, 2 * n + pair + 1)
                    if pair == 0 and mlp:
                        dve.wait_ge(weights_ready, n - 1)
                    steady(dve)
                    done = 0
                    two = [2 * pair, 2 * pair + 1]
                    for r in range(ROUNDS):
                        at = slice(8 * r, 8 * r + 8)
                        for x, e in enumerate(two):
                            if r:
                                dve.wait_ge(chain, done - 1 + x)
                            nc.vector.max(vals[:, par, e, at], keys[:, g, e, :]).then_inc(chain, 1)
                        done += 2
                        for x, e in enumerate(two):
                            dve.wait_ge(chain, done - 1 + x)
                            found = nc.vector.max_index(idx[:, par, e, at], vals[:, par, e, at], keys[:, g, e, :])
                            if r < ROUNDS - 1:
                                nc.vector.match_replace(keys[:, g, e, :], vals[:, par, e, at], keys[:, g, e, :],
                                                        NEG).then_inc(chain, 1)
                        if r < ROUNDS - 1:
                            done += 2
                    found.then_inc(chain, 1)
                    done += 1
                    dve.wait_ge(chain, done)
                    if pair == 0 and mlp:
                        invert(n - 1, 1 - par)
                    elif pair == 0:
                        nc.vector.drain()
                    else:
                        nc.vector.tensor_scalar(ntop[:, par, :], vals[:, par, :, 0], -1.0, None, ALU.mult)
                        if mlp:
                            dve.wait_ge(digits_out, 16 * n - 16)
                        src = idx[:, par].rearrange("p e r -> p (e r)").bitcast(U8).rearrange("p (n two) -> p n two", two=2)[:, :, 0]
                        nc.vector.tensor_scalar(digits[:, par, 0, :], src, LO - 1, None, ALU.bitwise_and)
                        nc.vector.tensor_scalar(digits[:, par, 1, :], src, 4, None, ALU.logical_shift_right).then_inc(ranked, 1)
                    dve.sem_clear(chain)

            slots(dve, slot)
            invert(TILES * BPT - 1, (BPT - 1) % 2)

        @block.scalar
        def _(act):
            def keys_out(t, gs):
                for g in gs:
                    for pair in range(2):
                        act.wait_ge(gated, 2 * (t * BPT + g) + pair + 1)
                        nc.scalar.activation(keys[:, g, 2 * pair:2 * pair + 2, :],
                                             ps[:, GATE_B, 0:2 * D].rearrange("p (e f) -> p e f", e=2),
                                             ACT.Copy).then_inc(keys_ready, 1)

            def make_table(t):
                act.wait_ge(split, t + 1)
                for j in range(PER):
                    ins = nc.scalar.activation(table[:, :, :, LO * j:LO * (j + 1)].rearrange("p s o l -> p (s o) l"),
                                               parts[:].rearrange("p s o l -> p (s o) l"), ACT.Copy, scale=own[:, j:j + 1])
                ins.then_inc(table_ready, 1)

            def slot(t, g, mlp):
                n, par = t * BPT + g, g % 2
                m = (g - 1) % BPT
                tm = t if g else t - 1
                units = units_of(m) if mlp else []
                spots = unit_spots(m)
                if g == 0:
                    keys_out(t, (2, 3))
                if g == 2 and not last_tile(t):
                    keys_out(t + 1, (0, 1))
                act.wait_ge(ranked, n + 1)
                if mlp:
                    act.wait_ge(weighted, n - 1)
                for e in range(GRP):
                    ins = nc.scalar.activation(ew[:, par, e, :], vals[:, par, e, :], ACT.Exp, bias=ntop[:, par, e:e + 1],
                                               accum_out=esum[:, par, e:e + 1])
                ins.then_inc(weights_ready, 1)

                def measure(q):
                    act.wait_ge(hi_in[q], 16 * n + 16)
                    at = slice(q * QO, (q + 1) * QO)
                    nc.scalar.activation(hot[:, at, :], hi_b[:, at, :], ACT.Abs, bias=colv[:, 6:7]).then_inc(distance, 1)

                def code(q):
                    act.wait_ge(distance, PIECES * n + q + 1)
                    at = slice(q * QO, (q + 1) * QO)
                    nc.scalar.activation(hot[:, at, :], hot[:, at, :], ACT.Relu, scale=-1.0, bias=1.0).then_inc(hot_ready, 1)

                measure(0)
                measure(1)
                code(0)
                code(1)
                for o in range(OCT):
                    if o == 4 or o == 8:
                        measure(o // 4 + 1)
                    if o == 5 or o == 9:
                        code(o // 4 + 1)
                    act.wait_ge(looked, OCT * n + o + 1)
                    if mlp or o >= 4:
                        act.wait_ge(picked_ready, OCT * n + o - 3)
                    nc.scalar.activation(looked_s[:, o % 4, :], ps[:, LOOK_B + o % 2, 0:COLS], ACT.Copy).then_inc(looked_out, 1)
                    if mlp and o == 1:
                        act.wait_ge(x_turned, n)
                        nc.scalar.activation(xwt[:], ps[0:TOP, XT_B, :].rearrange("p (e j) -> p e j", e=GRP),
                                             ACT.Copy).then_inc(xwt_ready, 1)
                    if mlp:
                        for (u, e, half), spot in zip(units, spots):
                            if spot == o:
                                activate(tm, u, e)
                if g == 3 and not last_tile(t):
                    make_table(t + 1)
                if mlp and m == BPT - 1:
                    final(tm)
                scale_out(n, par)

            def activate(tm, u, e):
                act.wait_ge(gate_up, UNITS * tm + u + 1)
                if u >= 2 or not isinstance(tm, int):
                    act.wait_ge(hidden, UNITS * tm + u - 1 if u else UNITS * tm)
                gu = ps[0:HALF, GU_B, :].rearrange("p (a c j) -> p a c j", a=2, c=2)
                nc.scalar.activation(gate_s[:, u % 2], gu[:, 0], ACT.Silu)
                nc.scalar.activation(up_s[:, u % 2], gu[:, 1], ACT.Copy).then_inc(activated, 1)

            def scale_out(n, par):
                act.wait_ge(placed, OCT * n + OCT)
                act.wait_ge(inverted, n + 1)
                for e in range(GRP):
                    ins = nc.scalar.activation(xs[:, e, :], ps[:, XG_B, e * TOP:(e + 1) * TOP], ACT.Copy,
                                               scale=einv[:, par, e:e + 1])
                ins.then_inc(scaled, 1)

            def final(t):
                act.wait_ge(downed, UNITS * t + UNITS)
                nc.scalar.activation(y[:], ps[:, Y_B, 0:D], ACT.Copy, accum_out=st[:, 0:1]).then_inc(y_out, 1)
                act.wait_ge(mean_ready, t + 1)
                nc.scalar.activation(ysq[:], y[:], ACT.Square, bias=st[:, 1:2], accum_out=st[:, 2:3]).then_inc(squared, 1)
                act.wait_ge(shift_ready, t + 1)
                nc.scalar.activation(yn[:], y[:], ACT.Identity, scale=st[:, 4:5], bias=st[:, 5:6]).then_inc(yn_ready, 1)
                act.wait_ge(y_turned, t + 1)
                for k in range(2):
                    ins = nc.scalar.activation(zt[:, k, :], ps[0:HALF, FIN_B, k * TILE:(k + 1) * TILE], ACT.Identity,
                                               scale=colv[:, 2 + k:3 + k], bias=colv[:, 4 + k:5 + k])
                ins.then_inc(zt_ready, 1)
                act.wait_ge(m1_done, t + 1)
                for k in range(2):
                    ins = nc.scalar.activation(st1[0:HALF, k, :], ps[0:HALF, FIN_B, (2 + k) * TILE:(3 + k) * TILE],
                                               ACT.Silu, bias=colv[:, k:k + 1])
                ins.then_inc(st1_ready, 1)
                act.wait_ge(m2_done, t + 1)
                act.wait_ge(fin_ready, t)
                nc.scalar.activation(m2s[:], ps[:, FIN_B, 0:D], ACT.Copy).then_inc(m2_out, 1)

            keys_out(0, (0, 1))
            make_table(0)
            slots(act, slot)
            tm = TILES - 1
            act.wait_ge(x_turned, TILES * BPT)
            nc.scalar.activation(xwt[:], ps[0:TOP, XT_B, :].rearrange("p (e j) -> p e j", e=GRP),
                                 ACT.Copy).then_inc(xwt_ready, 1)
            for u, e, half in units_of(BPT - 1):
                activate(tm, u, e)
            final(tm)

        @block.gpsimd
        def _(pool):
            def split_parts(t):
                pool.wait_ge(hr_in, 16 * PER * t + 16 * PER)
                if not (isinstance(t, int) and t == 0):
                    pool.wait_ge(table_ready, t)
                steady(pool)
                nc.gpsimd.tensor_copy(parts[:, 0], hr[:]).then_inc(rounded, 1)
                pool.wait_ge(rounded, 3 * t + 1)
                nc.gpsimd.tensor_tensor(rest[:], hr[:], parts[:, 0], ALU.subtract).then_inc(rounded, 1)
                pool.wait_ge(rounded, 3 * t + 2)
                steady(pool)
                nc.gpsimd.tensor_copy(parts[:, 1], rest[:]).then_inc(rounded, 1)
                pool.wait_ge(rounded, 3 * t + 3)
                nc.gpsimd.tensor_tensor(parts[:, 2], rest[:], parts[:, 1], ALU.subtract).then_inc(split, 1)

            def hide(tm, u):
                pool.wait_ge(activated, UNITS * tm + u + 1)
                if u >= 2 or not isinstance(tm, int):
                    pool.wait_ge(downed, UNITS * tm + u - 1 if u else UNITS * tm)
                nc.gpsimd.tensor_tensor(hid[:, u % 2], gate_s[:, u % 2], up_s[:, u % 2], ALU.mult).then_inc(hidden, 1)

            def slot(t, g, mlp):
                n, par = t * BPT + g, g % 2
                m = (g - 1) % BPT
                tm = t if g else t - 1
                units = units_of(m) if mlp else []
                spots = unit_spots(m)

                def mask(q):
                    pool.wait_ge(lo_in[q], 16 * n + 16)
                    steady(pool)
                    at = slice(q * QO, (q + 1) * QO)
                    nc.gpsimd.tensor_scalar(lomask[:, at, :], lo_b[:, at, :], lowv[:, 0:1], None,
                                            ALU.is_equal).then_inc(masked, 1)

                mask(0)
                for o in range(OCT):
                    if o % 4 == 2 and o < 12:
                        mask(o // 4 + 1)
                    pool.wait_ge(masked, PIECES * n + o // QO + 1)
                    pool.wait_ge(looked_out, OCT * n + o + 1)
                    if mlp or o >= 4:
                        pool.wait_ge(placed, OCT * n + o - 3)
                    nc.gpsimd.tensor_tensor(picked[:, o % 4, :], looked_s[:, o % 4, :], lomask[:, o, :],
                                            ALU.mult).then_inc(picked_ready, 1)
                    for (u, e, half), spot in zip(units, spots):
                        if spot == o and mlp:
                            hide(tm, u)
                if g == 3 and not last_tile(t):
                    split_parts(t + 1)
                if mlp and m == BPT - 1:
                    final(tm)
                pool.wait_ge(scaled, n + 1)
                if mlp:
                    pool.wait_ge(x_turned, n)
                nc.gpsimd.tensor_tensor(xw[:], xs[:], ew[:, par], ALU.mult).then_inc(weighted, 1)

            def final(t):
                pool.wait_ge(y_out, t + 1)
                steady(pool)
                nc.gpsimd.tensor_scalar(st[:, 1:2], st[:, 0:1], -1.0 / D, 0.0, ALU.mult, ALU.add).then_inc(mean_ready, 1)
                pool.wait_ge(squared, t + 1)
                steady(pool)
                nc.gpsimd.tensor_scalar(st[:, 3:4], st[:, 2:3], 1.0 / D, EPS2, ALU.mult, ALU.add).then_inc(var_ready, 1)
                pool.wait_ge(var_ready, t + 1)
                nc.gpsimd.tensor_tensor(st[:, 4:5], st[:, 3:4], lowv[:, 1:2], ALU.pow).then_inc(rstd_ready, 1)
                pool.wait_ge(rstd_ready, t + 1)
                nc.gpsimd.tensor_tensor(st[:, 5:6], st[:, 1:2], st[:, 4:5], ALU.mult).then_inc(shift_ready, 1)
                pool.wait_ge(m2_out, t + 1)
                pool.wait_ge(resid_in, 16 * t + 16)
                pool.wait_ge(out_done, 16 * t)
                nc.gpsimd.tensor_tensor(fin[:], m2s[:], resid[:], ALU.add).then_inc(fin_ready, 1)
                pool.wait_ge(fin_ready, t + 1)
                rows = TILE if last_tile(t) else STEP
                pool.dma_start(out[bass.ds(t * STEP, rows), :], fin[0:rows, :]).then_inc(out_done, 16)

            split_parts(0)
            slots(pool, slot)
            for u, e, half in units_of(BPT - 1):
                hide(TILES - 1, u)
            final(TILES - 1)

        @block.tensor
        def _(pe):
            def gates(t, gs):
                for g in gs:
                    for pair in range(2):
                        pe.wait_ge(keys_ready, 2 * (t * BPT + g) + pair)
                        for k in range(2):
                            ins = nc.tensor.matmul(ps[:, GATE_B, 0:2 * D], nt_gate[0:HALF + k, k, :],
                                                   wgate[0:HALF + k, k, GRP * g + 2 * pair:GRP * g + 2 * pair + 2, :],
                                                   start=(k == 0), stop=(k == 1))
                        ins.then_inc(gated, 1)

            def look(n, o, par, first):
                if o % QO == 0:
                    pe.wait_ge(hot_ready, PIECES * n + o // QO + 1)
                if not (first and o < 2):
                    pe.wait_ge(looked_out, OCT * n + o - 1)
                for s in range(3):
                    ins = nc.tensor.matmul(ps[:, LOOK_B + o % 2, 0:COLS], table[:, s, o, :], hot[:, o, :],
                                           start=(s == 0), stop=(s == 2))
                ins.then_inc(looked, 1)

            def put(n, o):
                if o == 0:
                    pe.wait_ge(scaled, n)
                pe.wait_ge(picked_ready, OCT * n + o + 1)
                nc.tensor.matmul(ps[:, XG_B, 0:COLS], place[:, OCT - 1 - o:OCT - 1 - o + TILE], picked[:, o % 4, :],
                                 start=(o == 0), stop=(o == OCT - 1)).then_inc(placed, 1)

            def turn_x(n):
                pe.wait_ge(weighted, n + 1)
                for e in range(GRP):
                    ins = nc.tensor.transpose(ps[0:TOP, XT_B, e * TILE:(e + 1) * TILE], xw[:, e, :], ident[:])
                ins.then_inc(x_turned, 1)

            def up(tm, u, e, half):
                if e is None and half == 0:
                    pe.wait_ge(nt_mlp_in, 16 * tm + 16)
                if e is not None and (e % GRP == 0):
                    pe.wait_ge(xwt_ready, BPT * tm + e // GRP + 1)
                pe.wait_ge(activated, UNITS * tm + u)
                for a in range(2):
                    for c in range(2):
                        dst = ps[0:HALF, GU_B, (2 * a + c) * TILE:(2 * a + c + 1) * TILE]
                        if e is None:
                            for k in range(2):
                                ins = nc.tensor.matmul(dst, wshared[:, k, 2 * a + half, c * HALF:(c + 1) * HALF], nt_mlp[:, k, :],
                                                       start=(k == 0), stop=(k == 1))
                        else:
                            at = a * D + c * HALF
                            ins = nc.tensor.matmul(dst, wexp[:, e, at:at + HALF], xwt[:, e % GRP, :], start=True, stop=True)
                ins.then_inc(gate_up, 1)

            def down(tm, u, e, half):
                if u == 0:
                    pe.wait_ge(y_out, tm)
                pe.wait_ge(hidden, UNITS * tm + u + 1)
                for c in range(2):
                    w = wsdown[:, 2 * half + c, :] if e is None else wdown[:, e, c, :]
                    ins = nc.tensor.matmul(ps[:, Y_B, 0:D], hid[:, u % 2, c, :], w, start=(u == 0 and c == 0),
                                           stop=(u == UNITS - 1 and c == 1))
                ins.then_inc(downed, 1)

            def final(t):
                pe.wait_ge(yn_ready, t + 1)
                for k in range(2):
                    ins = nc.tensor.transpose(ps[0:HALF, FIN_B, k * TILE:(k + 1) * TILE], yn[:, k * HALF:(k + 1) * HALF], ident[:])
                ins.then_inc(y_turned, 1)
                pe.wait_ge(zt_ready, t + 1)
                for c in range(2):
                    for k in range(2):
                        ins = nc.tensor.matmul(ps[0:HALF, FIN_B, (2 + c) * TILE:(3 + c) * TILE], wm1[:, k, c * HALF:(c + 1) * HALF],
                                               zt[:, k, :], start=(k == 0), stop=(k == 1))
                ins.then_inc(m1_done, 1)
                pe.wait_ge(st1_ready, t + 1)
                for k in range(2):
                    ins = nc.tensor.matmul(ps[:, FIN_B, 0:D], st1[0:HALF + k, k, :], wm2[0:HALF + k, k, :],
                                           start=(k == 0), stop=(k == 1))
                ins.then_inc(m2_done, 1)

            def slot(t, g, mlp):
                n, par = t * BPT + g, g % 2
                m = (g - 1) % BPT
                tm = t if g else t - 1
                units = units_of(m) if mlp else []
                spots = unit_spots(m)
                if g == 0:
                    gates(t, (2, 3))
                if g == 2 and not last_tile(t):
                    pe.wait_ge(nt_gate_in, 16 * (t + 1) + 16)
                    gates(t + 1, (0, 1))
                if g == 0:
                    pe.wait_ge(table_ready, t + 1)
                for o in range(OCT):
                    look(n, o, par, not mlp)
                    if o >= 3:
                        put(n, o - 3)
                    if mlp and o == 0:
                        turn_x(n - 1)
                    if mlp:
                        for (u, e, half), spot in zip(units, spots):
                            if spot == o:
                                up(tm, u, e, half)
                            if spot + 2 == o:
                                down(tm, u, e, half)
                for o in range(OCT - 3, OCT):
                    put(n, o)
                for (u, e, half), spot in zip(units, spots):
                    if spot + 2 >= OCT and mlp:
                        down(tm, u, e, half)
                if mlp and m == BPT - 1:
                    final(tm)

            pe.wait_ge(b_ones, 2)
            pe.wait_ge(nt_gate_in, 16)
            gates(0, (0, 1))
            slots(pe, slot)
            tm = TILES - 1
            turn_x(TILES * BPT - 1)
            rest_units = units_of(BPT - 1)
            for j, (u, e, half) in enumerate(rest_units):
                up(tm, u, e, half)
                if j:
                    down(tm, *rest_units[j - 1])
            down(tm, *rest_units[-1])
            final(tm)


def kernel(**inputs):
    import numpy as np
    import concourse.bacc as _bacc
    from concourse import mybir as _mybir
    from concourse.bass_utils import run_bass_kernel_spmd as _run

    g = {k: np.asarray(v) for k, v in inputs.items()}
    f32 = np.float32

    def halves(w, b=None):
        a = np.zeros((HALF + (b is not None), 2, w.shape[1]), f32)
        a[0:HALF, 0], a[0:HALF, 1] = w[0:HALF], w[HALF:D]
        if b is not None:
            a[HALF, 1] = b
        return a

    side = SIDE // PATCH
    patches = g["x"].reshape(IMAGES, CHANNELS, side, PATCH, side, PATCH).transpose(0, 1, 3, 5, 2, 4)
    patches = patches.reshape(IMAGES, PCH, 128, PATCHES).transpose(0, 2, 1, 3)
    w_patch = g["L0_tok_proj_w"].T.reshape(PCH, 128, D).transpose(1, 0, 2)

    wqkv, bqkv = g["L0_attn_w_qkv"], g["L0_attn_b_qkv"]
    w_pad = np.zeros((D, 2 * HG, 4, 32), f32)
    b_pad = np.zeros((2 * HG, 4, 32), f32)
    w_pad[..., 0:DH] = wqkv[:, 0:2 * D].reshape(D, 2 * HG, 4, DH)
    b_pad[..., 0:DH] = bqkv[0:2 * D].reshape(2 * HG, 4, DH)
    w_qk = halves(w_pad.reshape(D, -1), b_pad.reshape(-1)).reshape(HALF + 1, 2, 2 * HG, 128)

    p = np.arange(128)
    cols = np.zeros((128, 12), f32)
    for j, name in enumerate(("L0_ffn_m1_b", "L0_ffn_ln_g", "L0_ffn_ln_b")):
        cols[0:HALF, 2 * j:2 * j + 2] = g[name].reshape(2, HALF).T
    cols[0:HALF, 6] = -(np.arange(HALF) % HI)
    cols[:, 8] = p % LO
    cols[:, 9] = -0.5
    place = (np.arange(16 + 128)[None, :] == OCT * (p[:, None] // LO) + OCT - 1).astype(f32)
    own = (np.arange(PER)[None, :] == np.arange(HALF)[:, None] // HI).astype(f32)
    mask = np.zeros((TOK, 4, TOK), f32)
    mask[np.arange(1, TOK), :, np.arange(1, TOK)] = MASKED
    pos_t = halves(g["L0_ffn_posembed"].T, np.ones(EXPERTS, f32))

    arrays = dict(
        patches=patches, txt=g["txt"], w_patch=w_patch, b_patch=g["L0_tok_proj_b"][None, :], w_qk=w_qk,
        scale=g["L0_attn_scale"], w_v=halves(wqkv[:, 2 * D:], bqkv[2 * D:]),
        w_o=halves(g["L0_attn_w_proj"], g["L0_attn_b_proj"]),
        pos_t=pos_t, w_pos=halves(g["L0_ffn_pos_w"], g["L0_ffn_pos_b"]), w_gate=halves(g["L0_ffn_gate_w"]),
        b_gate=g["L0_ffn_gate_b"],
        w_shared=halves(np.concatenate([g["L0_ffn_sg_w"], g["L0_ffn_su_w"]], axis=1)).reshape(HALF, 2, 4, D),
        w_sdown=g["L0_ffn_sd_w"].reshape(4, HALF, D).transpose(1, 0, 2),
        w_exp=np.concatenate([g["L0_ffn_eg_w"], g["L0_ffn_eu_w"]], axis=2).transpose(1, 0, 2),
        w_down=g["L0_ffn_ed_w"].reshape(EXPERTS, 2, HALF, D).transpose(2, 0, 1, 3),
        w_m1=halves(g["L0_ffn_m1_w"]), w_m2=halves(g["L0_ffn_m2_w"], g["L0_ffn_m2_b"]), cols=cols,
        ident_in=np.eye(128, dtype=f32), place_in=place, own_in=own, mask_in=mask)

    nc = _bacc.Bacc("TRN2", target_bir_lowering=False, num_devices=1)
    args, maps = {}, {}
    for name, a in arrays.items():
        a = np.ascontiguousarray(a)
        maps[f"in_{name}"] = a
        args[name] = nc.dram_tensor(f"in_{name}", a.shape, _mybir.dt.from_np(a.dtype), kind="ExternalInput").ap()
    out = nc.dram_tensor("out_0", (TOKENS, D), F32, kind="ExternalOutput").ap()
    build(nc, out=out, **args)
    r = _run(nc, [maps], core_ids=[0])
    return r.results[0]["out_0"].reshape(IMAGES, TOK, D)
```

```python
from contextlib import ExitStack

import concourse.bass as bass
from concourse import mybir

F32 = mybir.dt.float32
BF16 = mybir.dt.bfloat16
U16 = mybir.dt.uint16
U8 = mybir.dt.uint8
ALU = mybir.AluOpType
ACT = mybir.ActivationFunctionType
AX_X = mybir.AxisListType.X

IMAGES, CHANNELS, SIDE, PATCH = 16, 3, 96, 16
PATCHES = (SIDE // PATCH) ** 2
TEXT = 77
TOK = PATCHES + TEXT
TOKENS = IMAGES * TOK
PDIM = CHANNELS * PATCH * PATCH
PCH = PDIM // 128
D = 192
HALF = D // 2
HEADS, DH = 12, 16
HG = HEADS // 4
EXPERTS = 16
TOP = D // 2
ROUNDS = TOP // 8
SHARED = 2 * D
GRP = 4
BPT = EXPERTS // GRP
COLS = GRP * TOP
TILE = 128
OCT = 16
PER = TILE // OCT
LO, HI = 16, D // 16
STEP = 120
TILES = (TOKENS - TILE) // STEP + 1
assert (TILES - 1) * STEP + TILE == TOKENS
KINDS = 2 * PER + 1
LOW_P = 32
UNITS = EXPERTS + SHARED // D
NEG = -3.0e38
MASKED = -1.0e30
EPS1, EPS2 = 1e-5, 1e-6


def build(nc, patches, txt, w_patch, b_patch, w_qk, scale, w_v, w_o, pos_t, w_pos, w_gate, b_gate, w_shared,
          w_sdown, w_exp, w_down, w_m1, w_m2, cols, ident_in, place_in, code_in, mask_in, out):
    tok_d = nc.dram_tensor("tok_d", [TOKENS, D], F32, kind="Internal").ap()
    norm_d = nc.dram_tensor("norm_d", [TOKENS, D], F32, kind="Internal").ap()
    normt_d = nc.dram_tensor("normt_d", [HALF, 2, TOKENS], F32, kind="Internal").ap()

    digit_d = nc.dram_tensor("digit_d", [2, 2, 2, TILE, COLS], BF16, kind="Internal").ap()

    with ExitStack() as ctx:
        def sb(name, shape, dt=F32):
            return ctx.enter_context(nc.sbuf_tensor(name, shape, dt))

        def sem(name):
            return ctx.enter_context(nc.semaphore(name))

        ident = sb("ident", [128, 128])
        wgate = sb("wgate", [HALF + 1, 2, EXPERTS, D])
        wshared = sb("wshared", [HALF, 2, 4, D])
        wsdown = sb("wsdown", [HALF, 4, D])
        wexp = sb("wexp", [TOP, EXPERTS, 2 * D])
        wdown = sb("wdown", [HALF, EXPERTS, 2, D])
        wm1 = sb("wm1", [HALF, 2, D])
        wm2 = sb("wm2", [HALF + 1, 2, D])
        colv = sb("colv", [HALF, 8])
        place = sb("place", [128, 16 + 128])
        powers = sb("powers", [128, 8])
        codef = sb("codef", [128, 2, 128])
        ps = ctx.enter_context(nc.psum_tensor("ps", [128, 8, 512], F32))

        consts_in = sem("consts_in")
        stored = sem("stored")
        consts = [(ident, ident_in), (wshared, w_shared), (wsdown, w_sdown), (wexp, w_exp), (wdown, w_down),
                  (wm1, w_m1), (wm2, w_m2), (colv, cols[0:HALF, 0:8]), (place, place_in),
                  (powers, cols[:, 8:16]), (codef, code_in)]
        CONSTS = 16 * len(consts)

        attention(nc, patches, txt, w_patch, b_patch, w_qk, scale, w_v, w_o, pos_t, w_pos, w_gate, b_gate, mask_in,
                  tok_d, norm_d, normt_d, ident, wgate, powers, ps, consts, consts_in, CONSTS, stored)
        experts(nc, sb, sem, tok_d, norm_d, normt_d, digit_d, out, ident, wgate, wshared, wsdown, wexp, wdown,
                wm1, wm2, colv, place, powers, codef, ps)


def attention(nc, patches, txt, w_patch, b_patch, w_qk, scale, w_v, w_o, pos_t, w_pos, w_gate, b_gate, mask_in,
              tok_d, norm_d, normt_d, ident, wgate, powers, ps, consts, consts_in, CONSTS, stored):
    with ExitStack() as ctx:
        def sb(name, shape, dt=F32):
            return ctx.enter_context(nc.sbuf_tensor(name, shape, dt))

        def sem(name):
            return ctx.enter_context(nc.semaphore(name))

        wpatch = sb("wpatch", [128, PCH, D])
        bpatch = sb("bpatch", [1, D])
        wqk = sb("wqk", [HALF + 1, 2, 2 * HG, 128])
        scl = sb("scl", [HALF + 1, HG, 4])
        wv = sb("wv", [HALF + 1, 2, D])
        wo = sb("wo", [HALF + 1, 2, D])
        post = sb("post", [HALF + 1, 2, EXPERTS])
        wpos = sb("wpos", [HALF + 1, 2, D])
        gatew = sb("gatew", [HALF, 2, D])
        pe_row = sb("pe_row", [EXPERTS, D])
        pe_col = sb("pe_col", [HALF, 2, EXPERTS])
        pstat = sb("pstat", [EXPERTS, 4])
        mask = sb("mask", [TOK, 4, TOK])
        maskb = sb("maskb", [TOK, 4, TOK], BF16)
        identb = sb("identb", [128, 128], BF16)
        ones = sb("ones", [1, 128])
        patch = sb("patch", [128, PCH, PATCHES])
        h = sb("h", [TOK, D])
        xn = sb("xn", [TOK, D])
        xt = sb("xt", [HALF + 1, 2, TOK])
        qt = sb("qt", [128, HG, TOK])
        kz = sb("kz", [128, HG, 4, TOK])
        v = sb("v", [TOK, D])
        prob = sb("prob", [TOK, HEADS, TOK])
        probt = sb("probt", [TOK, HEADS, TOK])
        o = sb("o", [TOK, D])
        ot = sb("ot", [HALF + 1, 2, TOK])
        h2 = sb("h2", [TOK, D])
        hs = sb("hs", [TOK, D])
        hst = sb("hst", [HALF, 2, TOK])
        bst = sb("bst", [TOK, 6])
        mv = sb("mv", [TOK, 2])
        bst2 = sb("bst2", [TOK, 6])
        mv2 = sb("mv2", [TOK, 2])
        ve = sb("ve", [TOK, 2])
        rstd = sb("rstd", [TOK, 2])
        nmax = sb("nmax", [TOK, HEADS])
        rsum = sb("rsum", [TOK, HEADS])
        rinv = sb("rinv", [TOK, HEADS])

        early_in = sem("early_in")
        zeroed = sem("zeroed")
        setup_pe = sem("setup_pe")
        setup_vec = sem("setup_vec")
        setup_act = sem("setup_act")
        patch_in = sem("patch_in")
        text_in = sem("text_in")
        embedded = sem("embedded")
        tokens_ready = sem("tokens_ready")
        stats1 = sem("stats1")
        var1 = sem("var1")
        ve1 = sem("ve1")
        rstd1 = sem("rstd1")
        normed = sem("normed")
        transposed = sem("transposed")
        xt_ready = sem("xt_ready")
        qkv_done = sem("qkv_done")
        q_ready = sem("q_ready")
        k_ready = sem("k_ready")
        v_ready = sem("v_ready")
        scored = sem("scored")
        max_ready = sem("max_ready")
        probs = sem("probs")
        probs_turned = sem("probs_turned")
        turned_act = sem("turned_act")
        turned_vec = sem("turned_vec")
        mixed = sem("mixed")
        rinv_ready = sem("rinv_ready")
        o_ready = sem("o_ready")
        ot_ready = sem("ot_ready")
        projected = sem("projected")
        h2_ready = sem("h2_ready")
        stats2 = sem("stats2")
        var2 = sem("var2")
        ve2 = sem("ve2")
        rstd2 = sem("rstd2")
        hs_ready = sem("hs_ready")
        hst_ready = sem("hst_ready")
        tok_out = sem("tok_out")
        norm_out = sem("norm_out")
        normt_out = sem("normt_out")

        early = [(wpatch, w_patch), (bpatch, b_patch), (wqk, w_qk), (scl, scale), (wv, w_v), (wo, w_o),
                 (post, pos_t), (wpos, w_pos), (gatew, w_gate), (mask, mask_in),
                 (wgate, b_gate)]
        EARLY = 16 * (len(early))

        passed = sem("passed")

        def steady(eng):
            eng.sem_inc(passed, 1)

        block = ctx.enter_context(nc.Block())

        @block.sync
        def _(sp):
            for dst, src in early:
                if dst is scl:
                    sp.dma_start(scl[:], bass.AP(tensor=scale.tensor, offset=0, ap=[[0, HALF + 1], [4, HG], [1, 4]])).then_inc(early_in, 16)
                elif dst is wgate:
                    sp.dma_start(wgate[HALF:HALF + 1, 1, :, :],
                                 bass.AP(tensor=b_gate.tensor, offset=0, ap=[[0, 1], [0, EXPERTS], [1, D]])).then_inc(early_in, 16)
                else:
                    sp.dma_start(dst[:], src).then_inc(early_in, 16)
            for dst, src in consts:
                sp.dma_start(dst[:], src).then_inc(consts_in, 16)
            with sp.Fori(0, IMAGES) as i:
                sp.wait_ge(embedded, i)
                sp.dma_start(patch[:], patches[i]).then_inc(patch_in, 16)
                sp.wait_ge(h2_ready, i)
                sp.dma_start(h[PATCHES:TOK, :], txt[i]).then_inc(text_in, 16)
                sp.wait_ge(h2_ready, i + 1)
                sp.dma_start(tok_d[bass.ds(i * TOK, TOK), :], h2[:]).then_inc(tok_out, 16)
                sp.wait_ge(hs_ready, i + 1)
                sp.dma_start(norm_d[bass.ds(i * TOK, TOK), :], hs[:]).then_inc(norm_out, 16)
                sp.wait_ge(hst_ready, i + 1)
                steady(sp)
                sp.dma_start(normt_d[:, :, bass.ds(i * TOK, TOK)], hst[:]).then_inc(normt_out, 16)
            sp.wait_ge(tok_out, 16 * IMAGES)
            sp.wait_ge(norm_out, 16 * IMAGES)
            sp.wait_ge(normt_out, 16 * IMAGES)

        @block.gpsimd
        def _(pool):
            nc.gpsimd.memset(kz[:], 0.0).then_inc(zeroed, 1)
            pool.wait_ge(consts_in, CONSTS)
            with pool.Fori(0, IMAGES) as i:
                for n, (var, ready, done, eps, m) in enumerate(((var1, ve1, rstd1, EPS1, mv), (var2, ve2, rstd2, EPS1, mv2))):
                    pool.wait_ge(var, i + 1)
                    steady(pool)
                    nc.gpsimd.tensor_scalar(ve[:, n:n + 1], m[:, 1:2], 1.0, eps, ALU.mult, ALU.add).then_inc(ready, 1)
                    pool.wait_ge(ready, i + 1)
                    nc.gpsimd.tensor_tensor(rstd[:, n:n + 1], ve[:, n:n + 1], powers[0:TOK, 0:1], ALU.pow).then_inc(done, 1)

        @block.scalar
        def _(act):
            act.wait_ge(early_in, EARLY)
            nc.scalar.activation(maskb[:], mask[:], ACT.Copy).then_inc(setup_act, 1)
            act.wait_ge(consts_in, CONSTS)
            nc.scalar.activation(identb[:], ident[:], ACT.Copy).then_inc(setup_act, 1)
            act.wait_ge(setup_vec, 2)
            nc.scalar.activation(pe_row[:], ps[0:EXPERTS, 0, 0:D], ACT.Exp, bias=pstat[:, 0:1],
                                 accum_out=pstat[:, 1:2]).then_inc(setup_act, 1)
            act.wait_ge(setup_pe, 2)
            nc.scalar.activation(pe_col[:], ps[0:HALF, 1, 0:2 * EXPERTS].rearrange("p (c e) -> p c e", c=2),
                                 ACT.Copy).then_inc(setup_act, 1)
            with act.Fori(0, IMAGES) as i:
                act.wait_ge(embedded, i + 1)
                act.wait_ge(h2_ready, i)
                nc.scalar.activation(h[0:PATCHES, :], ps[0:PATCHES, 0, 0:D], ACT.Copy).then_inc(tokens_ready, 1)
                act.wait_ge(transposed, 3 * i + 1)
                nc.scalar.activation(xt[0:HALF, :, :], turn_view(ps), ACT.Copy).then_inc(xt_ready, 1)
                act.wait_ge(qkv_done, 3 * i + 2)
                for j in range(2):
                    nc.scalar.activation(kz[32 * j:32 * j + 32, :, j, :], heads_view(ps[32 * j:32 * j + 32, 3, 0:HG * TOK]),
                                         ACT.Copy).then_inc(k_ready, 1)
                act.wait_ge(qkv_done, 3 * i + 3)
                nc.scalar.activation(v[:], ps[0:TOK, 4, 0:D], ACT.Copy).then_inc(v_ready, 1)
                act.wait_ge(max_ready, i + 1)
                for hd in range(HEADS):
                    ins = nc.scalar.activation(prob[:, hd, :], ps[0:TOK, 5 + hd // 4, (hd % 4) * TOK:(hd % 4 + 1) * TOK],
                                               ACT.Exp, bias=nmax[:, hd:hd + 1], accum_out=rsum[:, hd:hd + 1])
                    if hd % 4 == 3:
                        ins.then_inc(probs, 1)
                for c in (0, 2):
                    act.wait_ge(probs_turned, 3 * i + c + 1)
                    nc.scalar.activation(probt[:, 4 * c:4 * c + 4, :], quad_view(ps, 2 + c), ACT.Copy).then_inc(turned_act, 1)
                act.wait_ge(transposed, 3 * i + 2)
                nc.scalar.activation(ot[0:HALF, :, :], turn_view(ps), ACT.Copy).then_inc(ot_ready, 1)
                act.wait_ge(transposed, 3 * i + 3)
                act.wait_ge(normt_out, 16 * i)
                nc.scalar.activation(hst[:], turn_view(ps), ACT.Copy).then_inc(hst_ready, 1)

        @block.vector
        def _(dve):
            nc.vector.memset(xt[HALF:HALF + 1, :, :], 1.0).then_inc(zeroed, 1)
            nc.vector.memset(ot[HALF:HALF + 1, :, :], 1.0).then_inc(zeroed, 1)
            nc.vector.memset(ones[:], 1.0).then_inc(zeroed, 1)
            dve.wait_ge(early_in, EARLY)
            nc.vector.tensor_tensor(
                wqk[:, :, 0:HG, :].rearrange("p k c (h d) -> p k (c h) d", h=4),
                wqk[:, :, 0:HG, :].rearrange("p k c (h d) -> p k (c h) d", h=4),
                bass.AP(tensor=scl[:].tensor, offset=scl[:].offset,
                        ap=[list(scl[:].ap[0]), [0, 2], [1, HEADS], [0, 32]]), ALU.mult).then_inc(setup_vec, 1)
            dve.wait_ge(setup_pe, 1)
            nc.vector.tensor_reduce(pstat[:, 0:1], ps[0:EXPERTS, 0, 0:D], AX_X, ALU.max, negate=True).then_inc(setup_vec, 1)
            dve.wait_ge(setup_act, 3)
            nc.vector.reciprocal(pstat[:, 2:3], pstat[:, 1:2]).then_inc(setup_vec, 1)
            dve.wait_ge(setup_vec, 3)
            nc.vector.tensor_scalar(pe_row[:], pe_row[:], pstat[:, 2:3], None, ALU.mult).then_inc(setup_vec, 1)
            dve.wait_ge(setup_act, 4)
            for e in range(EXPERTS):
                for k in range(2):
                    nc.vector.tensor_scalar(wgate[0:HALF, k, e, :], gatew[:, k, :], pe_col[:, k, e:e + 1], None,
                                            ALU.mult).then_inc(setup_vec, 1)
            with dve.Fori(0, IMAGES) as i:
                def norm(src, bstats, m, stats, var, done, n, dst, ready):
                    nc.vector.bn_stats(bstats[:], src[:]).then_inc(stats, 1)
                    dve.wait_ge(stats, i + 1)
                    steady(dve)
                    nc.vector.bn_aggr(m[:], bstats[:]).then_inc(var, 1)
                    dve.wait_ge(done, i + 1)
                    nc.vector.tensor_scalar(dst[:], src[:], m[:, 0:1], rstd[:, n:n + 1], ALU.subtract,
                                            ALU.mult).then_inc(ready, 1)

                dve.wait_ge(tokens_ready, i + 1)
                dve.wait_ge(text_in, 16 * i + 16)
                norm(h, bst, mv, stats1, var1, rstd1, 0, xn, normed)
                dve.wait_ge(qkv_done, 3 * i + 1)
                nc.vector.tensor_copy(qt[:], ps[:, 2, 0:HG * TOK].rearrange("p (c j) -> p c j", c=HG)).then_inc(q_ready, 1)
                dve.wait_ge(qkv_done, 3 * i + 2)
                for j in range(2, 4):
                    nc.vector.tensor_copy(kz[32 * j:32 * j + 32, :, j, :],
                                          heads_view(ps[32 * j:32 * j + 32, 3, 0:HG * TOK])).then_inc(k_ready, 1)
                dve.wait_ge(scored, i + 1)
                nc.vector.tensor_reduce(nmax[:], ps[0:TOK, 5:8, 0:4 * TOK].rearrange("p c (h j) -> p c h j", h=4),
                                        AX_X, ALU.max, negate=True).then_inc(max_ready, 1)
                dve.wait_ge(probs_turned, 3 * i + 2)
                nc.vector.tensor_copy(probt[:, 4:8, :], quad_view(ps, 3)).then_inc(turned_vec, 1)
                dve.wait_ge(probs, 3 * i + 3)
                nc.vector.reciprocal(rinv[:], rsum[:]).then_inc(rinv_ready, 1)
                dve.wait_ge(rinv_ready, i + 1)
                dve.wait_ge(mixed, i + 1)
                nc.vector.tensor_tensor(o[:].rearrange("p (h d) -> p h d", h=HEADS),
                                        ps[0:TOK, 0, 0:D].rearrange("p (h d) -> p h d", h=HEADS),
                                        bass.AP(tensor=rinv[:].tensor, offset=rinv[:].offset,
                                                ap=[list(rinv[:].ap[0]), [1, HEADS], [0, DH]]),
                                        ALU.mult).then_inc(o_ready, 1)
                dve.wait_ge(projected, i + 1)
                dve.wait_ge(tok_out, 16 * i)
                nc.vector.tensor_tensor(h2[:], ps[0:TOK, 0, 256:256 + D], h[:], ALU.add).then_inc(h2_ready, 1)
                dve.wait_ge(h2_ready, i + 1)
                dve.wait_ge(norm_out, 16 * i)
                norm(h2, bst2, mv2, stats2, var2, rstd2, 1, hs, hs_ready)

        @block.tensor
        def _(pe):
            pe.wait_ge(early_in, EARLY)
            for k in range(2):
                last = nc.tensor.matmul(ps[0:EXPERTS, 0, 0:D], post[0:HALF + k, k, :], wpos[0:HALF + k, k, :],
                                        start=(k == 0), stop=(k == 1))
            last.then_inc(setup_pe, 1)
            pe.wait_ge(consts_in, CONSTS)
            pe.wait_ge(setup_vec, 4)
            for k in range(2):
                last = nc.tensor.transpose(ps[0:HALF, 1, EXPERTS * k:EXPERTS * (k + 1)], pe_row[:, HALF * k:HALF * (k + 1)],
                                           ident[0:EXPERTS, 0:EXPERTS])
            last.then_inc(setup_pe, 1)
            pe.wait_ge(setup_act, 4)
            pe.wait_ge(zeroed, 4)
            with pe.Fori(0, IMAGES) as i:
                def turn(src):
                    for k in range(2):
                        last = nc.tensor.transpose(ps[0:HALF, 1, 128 * k:128 * k + TOK], src[:, HALF * k:HALF * (k + 1)],
                                                   ident[0:TOK, 0:TOK])
                    last.then_inc(transposed, 1)

                pe.wait_ge(patch_in, 16 * i + 16)
                pe.wait_ge(h2_ready, i)
                for c in range(PCH):
                    nc.tensor.matmul(ps[0:PATCHES, 0, 0:D], patch[:, c, :], wpatch[:, c, :], start=(c == 0), stop=False)
                nc.tensor.matmul(ps[0:PATCHES, 0, 0:D], ones[0:1, 0:PATCHES], bpatch[:], start=False,
                                 stop=True).then_inc(embedded, 1)
                pe.wait_ge(normed, i + 1)
                pe.wait_ge(hst_ready, i)
                turn(xn)
                pe.wait_ge(xt_ready, i + 1)
                for w in range(2):
                    for c in range(HG):
                        for k in range(2):
                            last = nc.tensor.matmul(ps[:, 2 + w, c * TOK:(c + 1) * TOK], wqk[0:HALF + k, k, HG * w + c, :],
                                                    xt[0:HALF + k, k, :], start=(k == 0), stop=(k == 1))
                    last.then_inc(qkv_done, 1)
                for k in range(2):
                    last = nc.tensor.matmul(ps[0:TOK, 4, 0:D], xt[0:HALF + k, k, :], wv[0:HALF + k, k, :],
                                            start=(k == 0), stop=(k == 1))
                last.then_inc(qkv_done, 1)
                for c in range(HG):
                    nc.tensor.matmul(ps[0:TOK, 5 + c, 0:4 * TOK], identb[0:TOK, 0:TOK], maskb[:], start=True, stop=False)
                pe.wait_ge(q_ready, i + 1)
                pe.wait_ge(k_ready, 4 * i + 4)
                for c in range(HG):
                    last = nc.tensor.matmul(ps[0:TOK, 5 + c, 0:4 * TOK], qt[:, c, :], kz[:, c, :, :], start=False, stop=True)
                last.then_inc(scored, 1)
                pe.wait_ge(v_ready, i + 1)
                for c in range(HG):
                    pe.wait_ge(probs, 3 * i + c + 1)
                    for j in range(4):
                        last = nc.tensor.transpose(ps[0:TOK, 2 + c, j * TOK:(j + 1) * TOK], prob[:, 4 * c + j, :],
                                                   ident[0:TOK, 0:TOK])
                    last.then_inc(probs_turned, 1)
                pe.wait_ge(turned_act, 2 * i + 2)
                pe.wait_ge(turned_vec, i + 1)
                for hd in range(HEADS):
                    last = nc.tensor.matmul(ps[0:TOK, 0, hd * DH:(hd + 1) * DH], probt[:, hd, :], v[:, hd * DH:(hd + 1) * DH],
                                            start=True, stop=True)
                last.then_inc(mixed, 1)
                pe.wait_ge(o_ready, i + 1)
                turn(o)
                pe.wait_ge(ot_ready, i + 1)
                for k in range(2):
                    last = nc.tensor.matmul(ps[0:TOK, 0, 256:256 + D], ot[0:HALF + k, k, :], wo[0:HALF + k, k, :],
                                            start=(k == 0), stop=(k == 1))
                last.then_inc(projected, 1)
                pe.wait_ge(hs_ready, i + 1)
                turn(hs)


def turn_view(ps):
    return ps[0:HALF, 1, 0:256].rearrange("p (k j) -> p k j", k=2)[:, :, 0:TOK]


def heads_view(bank):
    return bank.rearrange("p (c j) -> p c j", c=HG)


def quad_view(ps, bank):
    return ps[0:TOK, bank, 0:4 * TOK].rearrange("p (h j) -> p h j", h=4)


FINAL_ACT = {1: 0, 3: 1, 5: 2, 8: 3, 12: 4}
FINAL_PE = {4: 0, 7: 1, 11: 2}
FINAL_POOL = {0: 0, 2: 1, 9: 2, 13: 3}
PREPARE = 9
MISC_B, LOOK_B, XG_B, GU_B, Y_B, CODE_B = 0, 1, 3, 4, 5, 6


def units_of(m):
    first = [(0, None, 0), (1, None, 1)] if m == 0 else []
    return first + [(2 + GRP * m + j, GRP * m + j, None) for j in range(GRP)]


def unit_spots(m):
    n = len(units_of(m))
    return [3 + 3 * j for j in range(n)] if n == 4 else [2 + 2 * j for j in range(n)]


def gate_spots():
    return {3: (0, 0), 6: (0, 1), 11: (1, 0), 14: (1, 1)}


def experts(nc, sb, sem, tok_d, norm_d, normt_d, digit_d, out, ident, wgate, wshared, wsdown, wexp, wdown,
            wm1, wm2, colv, place, powers, codef, ps):
    keys = sb("keys", [TILE, BPT, GRP, D])
    vals = sb("vals", [TILE, 2, GRP, TOP])
    idx = sb("idx", [TILE, 2, GRP, TOP], U16)
    digits = sb("digits", [TILE, 2, 2, COLS], U16)
    dcode = sb("dcode", [TILE, 2, 2, 2, COLS], BF16)
    rows = sb("rows", [128, 2, OCT, COLS], BF16)
    codew = sb("codew", [128, 2, 128], BF16)
    code = sb("code", [TILE, 4, 2, COLS], BF16)
    ntop = sb("ntop", [TILE, 2, GRP])
    esum = sb("esum", [TILE, 2, GRP])
    einv = sb("einv", [TILE, 2, GRP])
    ew = sb("ew", [TILE, 2, GRP, TOP])
    looked_s = sb("looked_s", [TILE, 4, COLS])
    picked = sb("picked", [TILE, 4, COLS])
    xs = sb("xs", [TILE, GRP, TOP])
    xw = sb("xw", [TILE, GRP, TOP])
    xwt = sb("xwt", [TOP, GRP, TILE])
    gu_s = sb("gu_s", [HALF, 2, 2, 2, TILE])
    tanh_s = sb("tanh_s", [HALF, 2, 2, TILE])
    prod_s = sb("prod_s", [HALF, 2, 2, TILE])
    turned_s = sb("turned_s", [HALF, 2, 2, TILE])
    hid = sb("hid", [HALF, 2, 2, TILE])
    nt_gate = sb("nt_gate", [HALF + 1, 2, TILE])
    nt_mlp = sb("nt_mlp", [HALF, 2, TILE])
    hr = sb("hr", [HALF, OCT, LO])
    rest = sb("rest", [HALF, OCT, LO])
    parts = sb("parts", [HALF, OCT, 3, LO], BF16)
    table = sb("table", [128, OCT, 3, TILE], BF16)
    resid = sb("resid", [TILE, D])
    y = sb("y", [TILE, D])
    ysq = sb("ysq", [TILE, D])
    yn = sb("yn", [TILE, D])
    st = sb("st", [TILE, 6])
    zt = sb("zt", [HALF, 2, TILE])
    st1 = sb("st1", [HALF + 1, 2, TILE])
    m2s = sb("m2s", [TILE, D])
    fin = sb("fin", [TILE, D])

    nt_gate_in, nt_mlp_in, hr_in, resid_in = sem("nt_gate_in"), sem("nt_mlp_in"), sem("hr_in"), sem("resid_in")
    b_ones, b_codew = sem("b_ones"), sem("b_codew")
    gated, keys_ready = sem("gated"), sem("keys_ready")
    chain = sem("chain")
    plain = sem("plain")
    ranked, coded, digits_out, rows_in = sem("ranked"), sem("coded"), sem("digits_out"), sem("rows_in")
    inverted = sem("inverted")
    weights_ready = sem("weights_ready")
    code_done, code_ready = sem("code_done"), sem("code_ready")
    rounded = sem("rounded")
    split, table_in = sem("split"), (sem("table_first_in"), sem("table_second_in"))
    looked, looked_out, picked_ready, placed = sem("looked"), sem("looked_out"), sem("picked_ready"), sem("placed")
    scaled, weighted, x_turned, xwt_ready = sem("scaled"), sem("weighted"), sem("x_turned"), sem("xwt_ready")
    gate_up, activated, half_hidden = sem("gate_up"), sem("activated"), sem("half_hidden")
    hidden, downed, biased = sem("hidden"), sem("downed"), sem("biased")
    y_out, mean_ready, squared, var_ready, rstd_ready = (sem("y_out"), sem("mean_ready"), sem("squared"),
                                                         sem("var_ready"), sem("rstd_ready"))
    shift_ready, yn_ready, y_turned, zt_ready = sem("shift_ready"), sem("yn_ready"), sem("y_turned"), sem("zt_ready")
    tanh_ready, half_st1 = sem("tanh_ready"), sem("half_st1")
    m1_done, st1_ready, m2_done, m2_out, fin_ready = (sem("m1_done"), sem("st1_ready"), sem("m2_done"),
                                                      sem("m2_out"), sem("fin_ready"))
    out_done = sem("out_done")
    passed = sem("passed")
    TABLE = 16 * PER

    def steady(eng):
        eng.sem_inc(passed, 1)

    def slots(eng, slot):
        slot(0, 0, False)
        slot(0, 1, True)
        slot(0, 2, True)
        with eng.Fori(0, TILES - 2) as t:
            slot(t, 3, True)
            for g in range(3):
                slot(t + 1, g, True)
        slot(TILES - 2, 3, True)
        for g in range(BPT):
            slot(TILES - 1, g, True)

    def last_tile(t):
        return isinstance(t, int) and t == TILES - 1

    def gates_of(t, g):
        if g % 2 == 0 or last_tile(t):
            return {}
        return {o: (g - 1 + b, pair) for o, (b, pair) in gate_spots().items()}

    def gated_before(t, g):
        return 2 * BPT * t + 2 * BPT + (4 if g in (2, 3) and not last_tile(t) else 0)

    with nc.Block() as block:

        @block.sync
        def _(sp):
            def load_gate(t):
                sp.dma_start(nt_gate[0:HALF, :, :], normt_d[:, :, bass.ds(t * STEP, TILE)]).then_inc(nt_gate_in, 16)
                for j in range(PER):
                    src = norm_d[bass.ds(t * STEP + j * OCT, OCT), :].rearrange("o (hi lo) -> hi o lo", lo=LO)
                    sp.dma_start(hr[HI * j:HI * (j + 1), :, :], src).then_inc(hr_in, 16)

            def load_mlp(t):
                sp.dma_start(nt_mlp[:], normt_d[:, :, bass.ds(t * STEP, TILE)]).then_inc(nt_mlp_in, 16)

            def build_table(t, part):
                sp.wait_ge(split, t + 1)
                if not (isinstance(t, int) and t == 0):
                    sp.wait_ge(looked, OCT * BPT * t - OCT // 2 * (1 - part))
                steady(sp)
                octs = slice(OCT // 2 * part, OCT // 2 * (part + 1))
                for j in range(PER):
                    sp.dma_start(table[HI * j:HI * (j + 1), octs, :, LO * j:LO * (j + 1)].rearrange("p o s l -> p (o s) l"),
                                 parts[HI * j:HI * (j + 1), octs].rearrange("p o s l -> p (o s) l")).then_inc(table_in[part], 16)

            load_gate(0)
            load_mlp(0)
            sp.wait_ge(b_ones, 4)
            build_table(0, 0)
            build_table(0, 1)

            def slot(t, g, mlp):
                n, par = t * BPT + g, g % 2
                if g == 1 and not last_tile(t):
                    sp.wait_ge(gated, 2 * BPT * t + 2 * BPT)
                    steady(sp)
                    sp.wait_ge(split, t + 1)
                    steady(sp)
                    load_gate(t + 1)
                sp.wait_ge(coded, n + 1)
                steady(sp)
                sp.dma_start(digit_d[par].rearrange("a k p c -> p a k c"), dcode[:, par]).then_inc(digits_out, 16)
                sp.wait_ge(digits_out, 16 * n + 16)
                steady(sp)
                if not isinstance(n, int) or n >= 2:
                    sp.wait_ge(code_done, OCT * n - OCT)
                    steady(sp)
                for a in range(2):
                    sp.dma_start(rows[LOW_P * a:LOW_P * a + 2 * PER, par, :, :],
                                 digit_d[par, a].rearrange("k (t o) c -> (k t) o c", o=OCT)).then_inc(rows_in, 16)
                if g == 0 and mlp:
                    build_table(t, 1)
                if g == 2 and not last_tile(t):
                    sp.wait_ge(gate_up, UNITS * t + 2)
                    steady(sp)
                    load_mlp(t + 1)
                if g == 3:
                    sp.wait_ge(fin_ready, t)
                    steady(sp)
                    sp.dma_start(resid[:], tok_d[bass.ds(t * STEP, TILE), :]).then_inc(resid_in, 16)
                    if not last_tile(t):
                        build_table(t + 1, 0)

            slots(sp, slot)
            sp.wait_ge(out_done, 16 * TILES)

        @block.vector
        def _(dve):
            nc.vector.memset(nt_gate[HALF:HALF + 1, :, :], 1.0).then_inc(b_ones, 1)
            nc.vector.memset(st1[HALF:HALF + 1, :, :], 2.0).then_inc(b_ones, 1)
            nc.vector.memset(rows[:], 1.0).then_inc(b_ones, 1)
            nc.vector.memset(table[:], 0.0).then_inc(b_ones, 1)

            def slot(t, g, mlp):
                n, par = t * BPT + g, g % 2
                for pair in range(2):
                    dve.wait_ge(keys_ready, 2 * n + pair + 1)
                    if pair == 0 and mlp:
                        dve.wait_ge(weights_ready, n - 1)
                    steady(dve)
                    done = 0
                    two = [2 * pair, 2 * pair + 1]
                    for r in range(ROUNDS):
                        at = slice(8 * r, 8 * r + 8)
                        for x, e in enumerate(two):
                            if r:
                                dve.wait_ge(chain, done - 1 + x)
                            nc.vector.max(vals[:, par, e, at], keys[:, g, e, :]).then_inc(chain, 1)
                        done += 2
                        for x, e in enumerate(two):
                            dve.wait_ge(chain, done - 1 + x)
                            found = nc.vector.max_index(idx[:, par, e, at], vals[:, par, e, at], keys[:, g, e, :])
                            if r < ROUNDS - 1:
                                nc.vector.match_replace(keys[:, g, e, :], vals[:, par, e, at], keys[:, g, e, :],
                                                        NEG).then_inc(chain, 1)
                        if r < ROUNDS - 1:
                            done += 2
                    found.then_inc(chain, 1)
                    done += 1
                    dve.wait_ge(chain, done)
                    if pair == 0:
                        nc.vector.drain()
                    else:
                        nc.vector.tensor_scalar(ntop[:, par, :], vals[:, par, :, 0], -1.0, None, ALU.mult)
                        if mlp:
                            dve.wait_ge(plain, n - 1)
                        src = idx[:, par].rearrange("p e r -> p (e r)")
                        nc.vector.tensor_scalar(digits[:, par, 0, :], src, 4, None, ALU.logical_shift_right)
                        nc.vector.tensor_scalar(digits[:, par, 1, :], src, LO - 1, None, ALU.bitwise_and).then_inc(ranked, 1)
                    dve.sem_clear(chain)

            slots(dve, slot)

        @block.scalar
        def _(act):
            def keys_out(t, g, pair):
                act.wait_ge(gated, 2 * (t * BPT + g) + pair + 1)
                nc.scalar.activation(keys[:, g, 2 * pair:2 * pair + 2, :],
                                     ps[:, MISC_B, 0:2 * D].rearrange("p (e f) -> p e f", e=2),
                                     ACT.Copy).then_inc(keys_ready, 1)

            def turned_out(n):
                act.wait_ge(x_turned, n + 1)
                nc.scalar.activation(xwt[:], ps[0:TOP, MISC_B, :].rearrange("p (e j) -> p e j", e=GRP),
                                     ACT.Copy).then_inc(xwt_ready, 1)

            def prepare(n, par):
                act.wait_ge(ranked, n + 1)
                if not isinstance(n, int) or n >= 2:
                    act.wait_ge(digits_out, 16 * n - 16)
                nc.scalar.activation(dcode[:, par, :, 1, :], digits[:, par, :, :], ACT.Copy).then_inc(plain, 1)
            def exponentials(n, par, e):
                if e == 0 and (not isinstance(n, int) or n >= 2):
                    act.wait_ge(weighted, n - 1)
                ins = nc.scalar.activation(ew[:, par, e, :], vals[:, par, e, :], ACT.Exp, bias=ntop[:, par, e:e + 1],
                                           accum_out=esum[:, par, e:e + 1])
                if e == GRP - 1:
                    ins.then_inc(weights_ready, 1)

            def code_out(n, o, first):
                act.wait_ge(code_done, OCT * n + o + 1)
                if not first or o >= 4:
                    act.wait_ge(picked_ready, OCT * n + o - 3)
                nc.scalar.activation(code[:, o % 4], ps[:, CODE_B:CODE_B + 2, 0:COLS], ACT.Relu).then_inc(code_ready, 1)

            def slot(t, g, mlp):
                n, par = t * BPT + g, g % 2
                m = (g - 1) % BPT
                tm = t if g else t - 1
                units = units_of(m) if mlp else []
                spots = unit_spots(m)
                gates = gates_of(t, g)
                for o in range(OCT):
                    act.wait_ge(looked, OCT * n + o + 1)
                    if mlp or o >= 4:
                        act.wait_ge(picked_ready, OCT * n + o - 3)
                    nc.scalar.activation(looked_s[:, o % 4, :], ps[:, LOOK_B + o % 2, 0:COLS], ACT.Copy).then_inc(looked_out, 1)
                    if o + 2 < OCT:
                        code_out(n, o + 2, not mlp)
                    if o == 1 and mlp:
                        turned_out(n - 1)
                    if o == PREPARE and not (last_tile(t) and g == BPT - 1):
                        prepare(n + 1, 1 - par)
                    if o > PREPARE and o - PREPARE <= GRP and not (last_tile(t) and g == BPT - 1):
                        exponentials(n + 1, 1 - par, o - PREPARE - 1)
                    if o in gates:
                        keys_out(t + 1, *gates[o])
                    for (u, e, half), spot in zip(units, spots):
                        if spot == o:
                            activate(tm, u, e)
                    if g == 2 and o in FINAL_ACT and not (isinstance(t, int) and t == 0):
                        final(t - 1, FINAL_ACT[o])
                if not (last_tile(t) and g == BPT - 1):
                    code_out(n + 1, 0, False)
                    code_out(n + 1, 1, False)
                scale_out(n, par)
                if mlp and m == BPT - 1:
                    y_taken(tm)

            def activate(tm, u, e):
                act.wait_ge(gate_up, UNITS * tm + u + 1)
                if u >= 2 or not isinstance(tm, int):
                    act.wait_ge(hidden, UNITS * tm + u - 1 if u else UNITS * tm)
                gu = ps[0:HALF, GU_B, :].rearrange("p (a c j) -> p a c j", a=2, c=2)
                nc.scalar.activation(tanh_s[:, u % 2], gu[:, 0], ACT.Tanh, scale=0.5)
                nc.scalar.activation(gu_s[:, u % 2], gu, ACT.Copy).then_inc(activated, 1)

            def scale_out(n, par):
                act.wait_ge(placed, OCT * n + OCT)
                act.wait_ge(inverted, n + 1)
                if not isinstance(n, int) or n >= 1:
                    act.wait_ge(weighted, n)
                for e in range(GRP):
                    ins = nc.scalar.activation(xs[:, e, :], ps[:, XG_B, e * TOP:(e + 1) * TOP], ACT.Copy,
                                               scale=einv[:, par, e:e + 1])
                ins.then_inc(scaled, 1)

            def y_taken(t):
                act.wait_ge(downed, UNITS * t + UNITS)
                if not (isinstance(t, int) and t == 0):
                    act.wait_ge(yn_ready, t)
                nc.scalar.activation(y[:], ps[:, Y_B, 0:D], ACT.Copy, scale=0.5, accum_out=st[:, 0:1]).then_inc(y_out, 1)

            def final(t, step):
                if step == 0:
                    act.wait_ge(mean_ready, t + 1)
                    nc.scalar.activation(ysq[:], y[:], ACT.Square, bias=st[:, 1:2], accum_out=st[:, 2:3]).then_inc(squared, 1)
                if step == 1:
                    act.wait_ge(shift_ready, t + 1)
                    nc.scalar.activation(yn[:], y[:], ACT.Identity, scale=st[:, 4:5], bias=st[:, 5:6]).then_inc(yn_ready, 1)
                if step == 2:
                    act.wait_ge(y_turned, t + 1)
                    for k in range(2):
                        ins = nc.scalar.activation(zt[:, k, :], ps[0:HALF, MISC_B, k * TILE:(k + 1) * TILE], ACT.Identity,
                                                   scale=colv[:, 2 + k:3 + k], bias=colv[:, 4 + k:5 + k])
                    ins.then_inc(zt_ready, 1)
                if step == 3:
                    act.wait_ge(m1_done, t + 1)
                    for k in range(2):
                        ins = nc.scalar.activation(st1[0:HALF, k, :], ps[0:HALF, MISC_B, (2 + k) * TILE:(3 + k) * TILE],
                                                   ACT.Identity, bias=colv[:, k:k + 1])
                    ins.then_inc(biased, 1)
                    act.wait_ge(biased, t + 1)
                    steady(act)
                    nc.scalar.activation(zt[:], st1[0:HALF], ACT.Tanh, scale=0.5).then_inc(tanh_ready, 1)
                if step == 4:
                    act.wait_ge(m2_done, t + 1)
                    if not (isinstance(t, int) and t == 0):
                        act.wait_ge(fin_ready, t)
                    nc.scalar.activation(m2s[:], ps[:, MISC_B, 0:D], ACT.Copy, scale=0.5).then_inc(m2_out, 1)

            nc.scalar.activation(codew[:], codef[:], ACT.Copy).then_inc(b_codew, 1)
            for g in range(BPT):
                for pair in range(2):
                    keys_out(0, g, pair)
            prepare(0, 0)
            for e in range(GRP):
                exponentials(0, 0, e)
            code_out(0, 0, True)
            code_out(0, 1, True)
            slots(act, slot)
            turned_out(TILES * BPT - 1)
            for u, e, half in units_of(BPT - 1):
                activate(TILES - 1, u, e)
            y_taken(TILES - 1)
            for step in range(5):
                final(TILES - 1, step)

        @block.gpsimd
        def _(pool):
            def split_part(t, step):
                if step == 0:
                    pool.wait_ge(hr_in, 16 * PER * t + 16 * PER)
                    if not (isinstance(t, int) and t == 0):
                        for half_in in table_in:
                            pool.wait_ge(half_in, TABLE * t)
                    steady(pool)
                    nc.gpsimd.tensor_copy(parts[:, :, 0, :], hr[:]).then_inc(rounded, 1)
                if step == 1:
                    pool.wait_ge(rounded, 3 * t + 1)
                    nc.gpsimd.tensor_tensor(rest[:], hr[:], parts[:, :, 0, :], ALU.subtract).then_inc(rounded, 1)
                if step == 2:
                    pool.wait_ge(rounded, 3 * t + 2)
                    steady(pool)
                    nc.gpsimd.tensor_copy(parts[:, :, 1, :], rest[:]).then_inc(rounded, 1)
                if step == 3:
                    pool.wait_ge(rounded, 3 * t + 3)
                    nc.gpsimd.tensor_tensor(parts[:, :, 2, :], rest[:], parts[:, :, 1, :], ALU.subtract).then_inc(split, 1)

            def hide(tm, u):
                pool.wait_ge(activated, UNITS * tm + u + 1)
                if u >= 2 or not isinstance(tm, int):
                    pool.wait_ge(downed, UNITS * tm + u - 1 if u else UNITS * tm)
                nc.gpsimd.tensor_tensor(prod_s[:, u % 2], gu_s[:, u % 2, 0], gu_s[:, u % 2, 1], ALU.mult).then_inc(half_hidden, 1)
                pool.wait_ge(half_hidden, 2 * UNITS * tm + 2 * u + 1)
                nc.gpsimd.tensor_tensor(turned_s[:, u % 2], prod_s[:, u % 2], tanh_s[:, u % 2], ALU.mult).then_inc(half_hidden, 1)
                pool.wait_ge(half_hidden, 2 * UNITS * tm + 2 * u + 2)
                nc.gpsimd.tensor_tensor(hid[:, u % 2], prod_s[:, u % 2], turned_s[:, u % 2], ALU.add).then_inc(hidden, 1)

            def square(n, par):
                pool.wait_ge(plain, n + 1)
                nc.gpsimd.tensor_tensor(dcode[:, par, :, 0, :], dcode[:, par, :, 1, :], dcode[:, par, :, 1, :],
                                        ALU.mult).then_inc(coded, 1)

            def slot(t, g, mlp):
                n, par = t * BPT + g, g % 2
                m = (g - 1) % BPT
                tm = t if g else t - 1
                units = units_of(m) if mlp else []
                spots = unit_spots(m)
                pool.wait_ge(weights_ready, n + 1)
                nc.gpsimd.tensor_tensor(einv[:, par, :], esum[:, par, :], powers[:, 4:8], ALU.pow).then_inc(inverted, 1)
                for o in range(OCT):
                    pool.wait_ge(looked_out, OCT * n + o + 1)
                    if mlp or o >= 4:
                        pool.wait_ge(placed, OCT * n + o - 3)
                    nc.gpsimd.tensor_tensor(picked[:, o % 4, :], looked_s[:, o % 4, :], code[:, o % 4, 1, :],
                                            ALU.mult).then_inc(picked_ready, 1)
                    if o == PREPARE and not (last_tile(t) and g == BPT - 1):
                        square(n + 1, 1 - par)
                    for (u, e, half), spot in zip(units, spots):
                        if spot == o:
                            hide(tm, u)
                    if g == 3 and not last_tile(t) and o in (1, 3, 5, 7):
                        split_part(t + 1, o // 2)
                    if g == 2 and mlp and o in FINAL_POOL and not (isinstance(t, int) and t == 0):
                        final(t - 1, FINAL_POOL[o])
                pool.wait_ge(scaled, n + 1)
                if mlp:
                    pool.wait_ge(x_turned, n)
                nc.gpsimd.tensor_tensor(xw[:], xs[:], ew[:, par], ALU.mult).then_inc(weighted, 1)

            def final(t, step):
                if step == 0:
                    pool.wait_ge(y_out, t + 1)
                    steady(pool)
                    nc.gpsimd.tensor_scalar(st[:, 1:2], st[:, 0:1], -1.0 / D, 0.0, ALU.mult, ALU.add).then_inc(mean_ready, 1)
                if step == 1:
                    pool.wait_ge(squared, t + 1)
                    steady(pool)
                    nc.gpsimd.tensor_scalar(st[:, 3:4], st[:, 2:3], 1.0 / D, EPS2, ALU.mult, ALU.add).then_inc(var_ready, 1)
                    pool.wait_ge(var_ready, t + 1)
                    nc.gpsimd.tensor_tensor(st[:, 4:5], st[:, 3:4], powers[:, 0:1], ALU.pow).then_inc(rstd_ready, 1)
                    pool.wait_ge(rstd_ready, t + 1)
                    nc.gpsimd.tensor_tensor(st[:, 5:6], st[:, 1:2], st[:, 4:5], ALU.mult).then_inc(shift_ready, 1)
                if step == 2:
                    pool.wait_ge(tanh_ready, t + 1)
                    nc.gpsimd.tensor_tensor(zt[:], zt[:], st1[0:HALF], ALU.mult).then_inc(half_st1, 1)
                    pool.wait_ge(half_st1, t + 1)
                    nc.gpsimd.tensor_tensor(st1[0:HALF], zt[:], st1[0:HALF], ALU.add).then_inc(st1_ready, 1)
                if step == 3:
                    pool.wait_ge(m2_out, t + 1)
                    pool.wait_ge(resid_in, 16 * t + 16)
                    if not (isinstance(t, int) and t == 0):
                        pool.wait_ge(out_done, 16 * t)
                    nc.gpsimd.tensor_tensor(fin[:], m2s[:], resid[:], ALU.add).then_inc(fin_ready, 1)
                    pool.wait_ge(fin_ready, t + 1)
                    rows_out = TILE if last_tile(t) else STEP
                    pool.dma_start(out[bass.ds(t * STEP, rows_out), :], fin[0:rows_out, :]).then_inc(out_done, 16)

            for step in range(4):
                split_part(0, step)
            square(0, 0)
            slots(pool, slot)
            for u, e, half in units_of(BPT - 1):
                hide(TILES - 1, u)
            for step in range(4):
                final(TILES - 1, step)

        @block.tensor
        def _(pe):
            def gate(t, g, pair):
                before = 2 * (t * BPT + g) + pair
                if not isinstance(before, int) or before:
                    pe.wait_ge(keys_ready, before)
                for k in range(2):
                    ins = nc.tensor.matmul(ps[:, MISC_B, 0:2 * D], nt_gate[0:HALF + k, k, :],
                                           wgate[0:HALF + k, k, GRP * g + 2 * pair:GRP * g + 2 * pair + 2, :],
                                           start=(k == 0), stop=(k == 1))
                ins.then_inc(gated, 1)

            def make_code(n, par, o, first):
                if not (first and o == 0):
                    pe.wait_ge(code_ready, OCT * n + o)
                for a in range(2):
                    ins = nc.tensor.matmul(ps[:, CODE_B + a, 0:COLS], codew[:, a, :], rows[:, par, o, :],
                                           start=True, stop=True)
                ins.then_inc(code_done, 1)

            def first_codes(n, par, o):
                if o == 0:
                    pe.wait_ge(rows_in, 32 * n + 32)
                make_code(n, par, o, isinstance(n, int) and n == 0)

            def look(n, o, first):
                pe.wait_ge(code_ready, OCT * n + o + 1)
                if not (first and o < 2):
                    pe.wait_ge(looked_out, OCT * n + o - 1)
                for s in range(3):
                    ins = nc.tensor.matmul(ps[:, LOOK_B + o % 2, 0:COLS], table[:, o, s, :], code[:, o % 4, 0, :],
                                           start=(s == 0), stop=(s == 2))
                ins.then_inc(looked, 1)

            def put(n, o, first):
                if o == 0 and not first:
                    pe.wait_ge(scaled, n)
                pe.wait_ge(picked_ready, OCT * n + o + 1)
                nc.tensor.matmul(ps[:, XG_B, 0:COLS], place[:, OCT - 1 - o:OCT - 1 - o + TILE], picked[:, o % 4, :],
                                 start=(o == 0), stop=(o == OCT - 1)).then_inc(placed, 1)

            def turn_x(n, t, g):
                pe.wait_ge(keys_ready, gated_before(t, g))
                if g == 3 and not (isinstance(t, int) and t == 0):
                    pe.wait_ge(m2_out, t)
                pe.wait_ge(weighted, n + 1)
                for e in range(GRP):
                    ins = nc.tensor.transpose(ps[0:TOP, MISC_B, e * TILE:(e + 1) * TILE], xw[:, e, :], ident[:])
                ins.then_inc(x_turned, 1)

            def up(tm, u, e, half):
                if e is None and half == 0:
                    pe.wait_ge(nt_mlp_in, 16 * tm + 16)
                if e is not None and (e % GRP == 0):
                    pe.wait_ge(xwt_ready, BPT * tm + e // GRP + 1)
                if u or not isinstance(tm, int):
                    pe.wait_ge(activated, UNITS * tm + u)
                for a in range(2):
                    for c in range(2):
                        dst = ps[0:HALF, GU_B, (2 * a + c) * TILE:(2 * a + c + 1) * TILE]
                        if e is None:
                            for k in range(2):
                                ins = nc.tensor.matmul(dst, wshared[:, k, 2 * a + half, c * HALF:(c + 1) * HALF], nt_mlp[:, k, :],
                                                       start=(k == 0), stop=(k == 1))
                        else:
                            at = a * D + c * HALF
                            ins = nc.tensor.matmul(dst, wexp[:, e, at:at + HALF], xwt[:, e % GRP, :], start=True, stop=True)
                ins.then_inc(gate_up, 1)

            def down(tm, u, e, half):
                if u == 0:
                    pe.wait_ge(y_out, tm)
                pe.wait_ge(hidden, UNITS * tm + u + 1)
                for c in range(2):
                    w = wsdown[:, 2 * half + c, :] if e is None else wdown[:, e, c, :]
                    ins = nc.tensor.matmul(ps[:, Y_B, 0:D], hid[:, u % 2, c, :], w, start=(u == 0 and c == 0),
                                           stop=(u == UNITS - 1 and c == 1))
                ins.then_inc(downed, 1)

            def final(t, step):
                if step == 0:
                    pe.wait_ge(yn_ready, t + 1)
                    for k in range(2):
                        ins = nc.tensor.transpose(ps[0:HALF, MISC_B, k * TILE:(k + 1) * TILE], yn[:, k * HALF:(k + 1) * HALF], ident[:])
                    ins.then_inc(y_turned, 1)
                if step == 1:
                    pe.wait_ge(zt_ready, t + 1)
                    for c in range(2):
                        for k in range(2):
                            ins = nc.tensor.matmul(ps[0:HALF, MISC_B, (2 + c) * TILE:(3 + c) * TILE],
                                                   wm1[:, k, c * HALF:(c + 1) * HALF], zt[:, k, :], start=(k == 0), stop=(k == 1))
                    ins.then_inc(m1_done, 1)
                if step == 2:
                    pe.wait_ge(st1_ready, t + 1)
                    for k in range(2):
                        ins = nc.tensor.matmul(ps[:, MISC_B, 0:D], st1[0:HALF + k, k, :], wm2[0:HALF + k, k, :],
                                               start=(k == 0), stop=(k == 1))
                    ins.then_inc(m2_done, 1)

            def slot(t, g, mlp):
                n, par = t * BPT + g, g % 2
                m = (g - 1) % BPT
                tm = t if g else t - 1
                units = units_of(m) if mlp else []
                spots = unit_spots(m)
                gates = gates_of(t, g)
                if g == 1 and not last_tile(t):
                    pe.wait_ge(nt_gate_in, 16 * (t + 1) + 16)
                for o in range(OCT):
                    if g == 0 and o in (0, OCT // 2):
                        pe.wait_ge(table_in[1 if o else 0], TABLE * t + TABLE)
                    look(n, o, not mlp)
                    if o == 1 and mlp:
                        turn_x(n - 1, t, g)
                    if o + 2 < OCT:
                        make_code(n, par, o + 2, False)
                    if o >= 3:
                        put(n, o - 3, not mlp)
                    if o in gates:
                        gb, pair = gates[o]
                        if gb == g - 1 and pair == 0 and mlp:
                            pe.wait_ge(xwt_ready, n)
                        gate(t + 1, gb, pair)
                    for (u, e, half), spot in zip(units, spots):
                        if spot == o:
                            up(tm, u, e, half)
                        if spot + 2 == o:
                            down(tm, u, e, half)
                    if g == 2 and o in FINAL_PE and not (isinstance(t, int) and t == 0):
                        final(t - 1, FINAL_PE[o])
                more = not (last_tile(t) and g == BPT - 1)
                if more:
                    first_codes(n + 1, 1 - par, 0)
                put(n, OCT - 3, False)
                put(n, OCT - 2, False)
                if more:
                    first_codes(n + 1, 1 - par, 1)
                put(n, OCT - 1, False)
                for (u, e, half), spot in zip(units, spots):
                    if spot + 2 >= OCT:
                        down(tm, u, e, half)

            pe.wait_ge(b_ones, 3)
            pe.wait_ge(b_codew, 1)
            pe.wait_ge(nt_gate_in, 16)
            for g in range(BPT):
                for pair in range(2):
                    gate(0, g, pair)
            first_codes(0, 0, 0)
            first_codes(0, 0, 1)
            slots(pe, slot)
            tm = TILES - 1
            turn_x(TILES * BPT - 1, TILES - 1, 3)
            rest_units = units_of(BPT - 1)
            for j, (u, e, half) in enumerate(rest_units):
                up(tm, u, e, half)
                if j:
                    down(tm, *rest_units[j - 1])
            down(tm, *rest_units[-1])
            for step in range(3):
                final(tm, step)


def kernel(**inputs):
    import numpy as np
    import concourse.bacc as _bacc
    from concourse import mybir as _mybir
    from concourse.bass_utils import run_bass_kernel_spmd as _run

    g = {k: np.asarray(v) for k, v in inputs.items()}
    f32 = np.float32

    def halves(w, b=None):
        a = np.zeros((HALF + (b is not None), 2, w.shape[1]), f32)
        a[0:HALF, 0], a[0:HALF, 1] = w[0:HALF], w[HALF:D]
        if b is not None:
            a[HALF, 1] = b
        return a

    side = SIDE // PATCH
    patches = g["x"].reshape(IMAGES, CHANNELS, side, PATCH, side, PATCH).transpose(0, 1, 3, 5, 2, 4)
    patches = patches.reshape(IMAGES, PCH, 128, PATCHES).transpose(0, 2, 1, 3)
    w_patch = g["L0_tok_proj_w"].T.reshape(PCH, 128, D).transpose(1, 0, 2)

    wqkv, bqkv = g["L0_attn_w_qkv"], g["L0_attn_b_qkv"]
    w_pad = np.zeros((D, 2 * HG, 4, 32), f32)
    b_pad = np.zeros((2 * HG, 4, 32), f32)
    w_pad[..., 0:DH] = wqkv[:, 0:2 * D].reshape(D, 2 * HG, 4, DH)
    b_pad[..., 0:DH] = bqkv[0:2 * D].reshape(2 * HG, 4, DH)
    w_qk = halves(w_pad.reshape(D, -1), b_pad.reshape(-1)).reshape(HALF + 1, 2, 2 * HG, 128)

    p = np.arange(128)
    cols = np.zeros((128, 16), f32)
    for j, name in enumerate(("L0_ffn_m1_b", "L0_ffn_ln_g", "L0_ffn_ln_b")):
        cols[0:HALF, 2 * j:2 * j + 2] = g[name].reshape(2, HALF).T
    cols[:, 8] = -0.5
    cols[:, 12:16] = -1.0
    code = np.zeros((128, 2, 128), f32)
    for a, n in enumerate((HI, LO)):
        for c in range(PER * n):
            at = LOW_P * a + c // n
            code[at, a, c], code[at + PER, a, c], code[LOW_P * a + 2 * PER, a, c] = -1.0, 2.0 * (c % n), 1.0 - (c % n) ** 2
    place = (np.arange(16 + 128)[None, :] == OCT * (p[:, None] // LO) + OCT - 1).astype(f32)
    mask = np.zeros((TOK, 4, TOK), f32)
    mask[np.arange(1, TOK), :, np.arange(1, TOK)] = MASKED
    pos_t = halves(g["L0_ffn_posembed"].T, np.ones(EXPERTS, f32))

    arrays = dict(
        patches=patches, txt=g["txt"], w_patch=w_patch, b_patch=g["L0_tok_proj_b"][None, :], w_qk=w_qk,
        scale=g["L0_attn_scale"], w_v=halves(wqkv[:, 2 * D:], bqkv[2 * D:]),
        w_o=halves(g["L0_attn_w_proj"], g["L0_attn_b_proj"]),
        pos_t=pos_t, w_pos=halves(g["L0_ffn_pos_w"], g["L0_ffn_pos_b"]), w_gate=halves(g["L0_ffn_gate_w"]),
        b_gate=g["L0_ffn_gate_b"],
        w_shared=halves(np.concatenate([g["L0_ffn_sg_w"], g["L0_ffn_su_w"]], axis=1)).reshape(HALF, 2, 4, D),
        w_sdown=g["L0_ffn_sd_w"].reshape(4, HALF, D).transpose(1, 0, 2),
        w_exp=np.concatenate([g["L0_ffn_eg_w"], g["L0_ffn_eu_w"]], axis=2).transpose(1, 0, 2),
        w_down=g["L0_ffn_ed_w"].reshape(EXPERTS, 2, HALF, D).transpose(2, 0, 1, 3),
        w_m1=halves(g["L0_ffn_m1_w"]), w_m2=halves(g["L0_ffn_m2_w"], g["L0_ffn_m2_b"]), cols=cols,
        ident_in=np.eye(128, dtype=f32), place_in=place, code_in=code, mask_in=mask)

    nc = _bacc.Bacc("TRN2", target_bir_lowering=False, num_devices=1)
    args, maps = {}, {}
    for name, a in arrays.items():
        a = np.ascontiguousarray(a)
        maps[f"in_{name}"] = a
        args[name] = nc.dram_tensor(f"in_{name}", a.shape, _mybir.dt.from_np(a.dtype), kind="ExternalInput").ap()
    out = nc.dram_tensor("out_0", (TOKENS, D), F32, kind="ExternalOutput").ap()
    build(nc, out=out, **args)
    r = _run(nc, [maps], core_ids=[0])
    return r.results[0]["out_0"].reshape(IMAGES, TOK, D)
```

```python
from contextlib import ExitStack

import concourse.bass as bass
from concourse import mybir

F32 = mybir.dt.float32
BF16 = mybir.dt.bfloat16
U16 = mybir.dt.uint16
U8 = mybir.dt.uint8
ALU = mybir.AluOpType
ACT = mybir.ActivationFunctionType
AX_X = mybir.AxisListType.X

IMAGES, CHANNELS, SIDE, PATCH = 16, 3, 96, 16
PATCHES = (SIDE // PATCH) ** 2
TEXT = 77
TOK = PATCHES + TEXT
TOKENS = IMAGES * TOK
PDIM = CHANNELS * PATCH * PATCH
PCH = PDIM // 128
D = 192
HALF = D // 2
HEADS, DH = 12, 16
HG = HEADS // 4
EXPERTS = 16
TOP = D // 2
ROUNDS = TOP // 8
SHARED = 2 * D
GRP = 4
BPT = EXPERTS // GRP
COLS = GRP * TOP
TILE = 128
OCT = 16
PER = TILE // OCT
LO, HI = 16, D // 16
TILES = TOKENS // TILE
REST = TOKENS - TILES * TILE
PACK = TILE // REST
BANDS = EXPERTS // PACK
assert REST == OCT and PACK == PER
KINDS = 2 * PER + 1
LOW_P = 32
REST_UNITS = SHARED // D + BANDS
UNITS = EXPERTS + SHARED // D
NEG = -3.0e38
MASKED = -1.0e30
EPS1, EPS2 = 1e-5, 1e-6


def build(nc, patches, txt, w_patch, b_patch, w_qk, scale, w_v, w_o, pos_t, w_pos, w_gate, b_gate, w_shared,
          w_sdown, w_exp, w_down, w_m1, w_m2, cols, ident_in, place_in, code_in, mask_in, out):
    tok_d = nc.dram_tensor("tok_d", [TOKENS, D], F32, kind="Internal").ap()
    norm_d = nc.dram_tensor("norm_d", [TOKENS, D], F32, kind="Internal").ap()
    normt_d = nc.dram_tensor("normt_d", [HALF, 2, TOKENS], F32, kind="Internal").ap()

    digit_d = nc.dram_tensor("digit_d", [2, 2, 2, TILE, COLS], BF16, kind="Internal").ap()

    with ExitStack() as ctx:
        def sb(name, shape, dt=F32):
            return ctx.enter_context(nc.sbuf_tensor(name, shape, dt))

        def sem(name):
            return ctx.enter_context(nc.semaphore(name))

        ident = sb("ident", [128, 128])
        wgate = sb("wgate", [HALF + 1, 2, EXPERTS, D])
        wshared = sb("wshared", [HALF, 2, 4, D])
        wsdown = sb("wsdown", [HALF, 4, D])
        wexp = sb("wexp", [TOP, EXPERTS, 2 * D])
        wdown = sb("wdown", [HALF, EXPERTS, 2, D])
        gatew = sb("gatew", [HALF + 1, 2, D])
        pe_col = sb("pe_col", [HALF, 2, EXPERTS])
        rows = sb("rows", [128, 2, OCT, COLS], BF16)
        table = sb("table", [128, OCT, 3, TILE], BF16)
        wm1 = sb("wm1", [HALF, 2, D])
        wm2 = sb("wm2", [HALF + 1, 2, D])
        colv = sb("colv", [HALF, 8])
        place = sb("place", [128, 16 + 128])
        powers = sb("powers", [128, 8])
        codef = sb("codef", [128, 2, 128])
        ps = ctx.enter_context(nc.psum_tensor("ps", [128, 8, 512], F32))

        late_in = sem("late_in")
        late = [(wexp, w_exp), (wdown, w_down), (wshared, w_shared), (wsdown, w_sdown), (wm1, w_m1), (wm2, w_m2),
                (colv, cols[0:HALF, 0:8]), (place, place_in), (codef, code_in)]

        attention(nc, patches, txt, w_patch, b_patch, w_qk, scale, w_v, w_o, pos_t, w_pos, w_gate, b_gate, mask_in,
                  tok_d, norm_d, normt_d, ident, wgate, gatew, pe_col, rows, table, powers, ps, late, late_in,
                  [(ident, ident_in), (powers, cols[:, 8:16])])
        experts(nc, sb, sem, tok_d, norm_d, normt_d, digit_d, out, ident, wgate, gatew, pe_col, rows, table, wshared, wsdown, wexp, wdown,
                wm1, wm2, colv, place, powers, codef, ps)


def attention(nc, patches, txt, w_patch, b_patch, w_qk, scale, w_v, w_o, pos_t, w_pos, w_gate, b_gate, mask_in,
              tok_d, norm_d, normt_d, ident, wgate, gatew, pe_col, rows, table, powers, ps, late, late_in, early_consts):
    with ExitStack() as ctx:
        def sb(name, shape, dt=F32):
            return ctx.enter_context(nc.sbuf_tensor(name, shape, dt))

        def sem(name):
            return ctx.enter_context(nc.semaphore(name))

        wpatch = sb("wpatch", [128, PCH, D])
        bpatch = sb("bpatch", [1, D])
        wqk = sb("wqk", [128, 2, 2 * HG, 128])
        scl = sb("scl", [128, HG, 4])
        wv = sb("wv", [128, 2, D])
        wo = sb("wo", [128, 2, D])
        post = sb("post", [HALF + 1, 2, EXPERTS])
        wpos = sb("wpos", [HALF + 1, 2, D])
        pe_row = sb("pe_row", [EXPERTS, D])
        pstat = sb("pstat", [EXPERTS, 4])
        mask = sb("mask", [TOK, 4, TOK])
        maskb = sb("maskb", [TOK, 4, TOK], BF16)
        identb = sb("identb", [128, 128], BF16)
        ones = sb("ones", [1, 128])
        fill = sb("fill", [128, 2, COLS], BF16)
        patch = sb("patch", [128, 2, PCH, PATCHES])
        h = sb("h", [TOK, 2, D])
        hkept = sb("hkept", [TOK, 2, D])
        xn = sb("xn", [TOK, D])
        xt = sb("xt", [128, 2, TOK])
        qt = sb("qt", [128, HG, TOK])
        kz = sb("kz", [128, HG, 4, TOK])
        v = sb("v", [TOK, D])
        prob = sb("prob", [TOK, HEADS, TOK])
        probt = sb("probt", [TOK, HEADS, TOK])
        o = sb("o", [TOK, D])
        ot = sb("ot", [128, 2, TOK])
        h2 = sb("h2", [TOK, D])
        hs = sb("hs", [TOK, D])
        hst = sb("hst", [HALF, 2, TOK])
        bst = sb("bst", [TOK, 6])
        mv = sb("mv", [TOK, 2])
        bst2 = sb("bst2", [TOK, 6])
        mv2 = sb("mv2", [TOK, 2])
        ve = sb("ve", [TOK, 2])
        rstd = sb("rstd", [TOK, 2])
        nmax = sb("nmax", [TOK, HEADS])
        rsum = sb("rsum", [TOK, HEADS])
        rinv = sb("rinv", [TOK, HEADS])

        early_in = sem("early_in")
        zeroed, filled = sem("zeroed"), sem("filled")
        setup_pe = sem("setup_pe")
        setup_vec = sem("setup_vec")
        setup_act = sem("setup_act")
        patch_in = (sem("even_patch_in"), sem("odd_patch_in"))
        text_in = (sem("even_text_in"), sem("odd_text_in"))
        embedded, tokens_ready, kept = sem("embedded"), sem("tokens_ready"), sem("kept")
        stats1, var1, ve1, rstd1, normed = sem("stats1"), sem("var1"), sem("ve1"), sem("rstd1"), sem("normed")
        x_turned, xt_ready = sem("x_turned"), sem("xt_ready")
        q_done, q_ready = sem("q_done"), sem("q_ready")
        k_done, k_ready = sem("k_done"), sem("k_ready")
        v_done, v_ready = sem("v_done"), sem("v_ready")
        scored, max_ready = sem("scored"), sem("max_ready")
        probs = sem("probs")
        probs_turned = sem("probs_turned")
        turned_act, turned_vec = sem("turned_act"), sem("turned_vec")
        mixed, rinv_ready, o_ready = sem("mixed"), sem("rinv_ready"), sem("o_ready")
        o_turned, ot_ready = sem("o_turned"), sem("ot_ready")
        projected, h2_ready = sem("projected"), sem("h2_ready")
        stats2, var2, ve2, rstd2, hs_ready = sem("stats2"), sem("var2"), sem("ve2"), sem("rstd2"), sem("hs_ready")
        hs_turned, hst_ready = sem("hs_turned"), sem("hst_ready")
        tok_out, norm_out, normt_out = sem("tok_out"), sem("norm_out"), sem("normt_out")
        passed = sem("passed")

        EMBED_B, Q_B, K_B, SCORE_B, OUT_B, V_B = 0, 1, 2, 3, 6, 7
        early = early_consts + [(wpatch, w_patch), (bpatch, b_patch), (wqk, w_qk), (scl, scale), (wv, w_v), (wo, w_o),
                                (post, pos_t), (wpos, w_pos), (gatew, w_gate), (mask, mask_in), (wgate, b_gate)]
        EARLY = 16 * len(early)

        def steady(eng):
            eng.sem_inc(passed, 1)

        def slots(eng, slot):
            slot(0, 0, 0, None, None)
            slot(1, 1, 1, 0, None)
            slot(2, 0, 2, 1, 0)
            slot(3, 1, 3, 2, 1)
            with eng.Fori(2, IMAGES // 2 - 1) as pair:
                for par in range(2):
                    k = pair * 2 + par
                    slot(k, par, k, k - 1, k - 2)
            slot(IMAGES - 2, 0, IMAGES - 2, IMAGES - 3, IMAGES - 4)
            slot(IMAGES - 1, 1, IMAGES - 1, IMAGES - 2, IMAGES - 3)
            slot(IMAGES, 0, None, IMAGES - 1, IMAGES - 2)
            slot(IMAGES + 1, 1, None, None, IMAGES - 1)

        def among(i):
            return not isinstance(i, int) or i < IMAGES

        def loads(i, par):
            return 8 * (i - par) + 16

        def later(i):
            return not (isinstance(i, int) and i == 0)

        def turn_view(bank):
            return ps[0:HALF, bank, 256:512].rearrange("p (k j) -> p k j", k=2)[:, :, 0:TOK]

        def out_view():
            return ps[0:HALF, OUT_B, 0:256].rearrange("p (k j) -> p k j", k=2)[:, :, 0:TOK]

        def heads_view(bank):
            return bank.rearrange("p (c j) -> p c j", c=HG)

        def quad_view(c):
            return ps[0:TOK, SCORE_B + c, 0:4 * TOK].rearrange("p (h j) -> p h j", h=4)

        block = ctx.enter_context(nc.Block())

        @block.sync
        def _(sp):
            def load_patches(a, par):
                if not isinstance(a, int) or a >= 2:
                    sp.wait_ge(embedded, a - 1)
                    steady(sp)
                sp.dma_start(patch[:, par], patches[a]).then_inc(patch_in[par], 16)

            def load_text(a, par):
                if not isinstance(a, int) or a >= 2:
                    sp.wait_ge(kept, a - 1)
                    steady(sp)
                    sp.wait_ge(normed, a - 1)
                    steady(sp)
                sp.dma_start(h[PATCHES:TOK, par, :], txt[a]).then_inc(text_in[par], 16)

            for dst, src in early:
                if dst is scl:
                    sp.dma_start(scl[:], bass.AP(tensor=scale.tensor, offset=0, ap=[[0, 128], [4, HG], [1, 4]])).then_inc(early_in, 16)
                elif dst is wgate:
                    sp.dma_start(wgate[HALF:HALF + 1, 1, :, :],
                                 bass.AP(tensor=b_gate.tensor, offset=0, ap=[[0, 1], [0, EXPERTS], [1, D]])).then_inc(early_in, 16)
                else:
                    sp.dma_start(dst[:], src).then_inc(early_in, 16)
            load_patches(0, 0)
            load_text(0, 0)
            load_patches(1, 1)
            def load_late(k):
                if k == 0:
                    for dst, src in late[2:]:
                        sp.dma_start(dst[:], src).then_inc(late_in, 16)
                if k in (1, IMAGES - 2):
                    dst, src = late[0 if k == 1 else 1]
                    sp.dma_start(dst[:], src).then_inc(late_in, 16)
                if k in (IMAGES - 1, IMAGES):
                    sp.wait_ge(filled, 2)
                    which = k - (IMAGES - 1)
                    dst = (rows[:].rearrange("p a o c -> p (a o) c"), table[:].rearrange("p o s j -> p o (s j)"))[which]
                    src = fill[:, which, :]
                    sp.dma_start(dst, bass.AP(tensor=src.tensor, offset=src.offset,
                                              ap=[list(src.ap[0]), [0, dst.shape[1]], [1, COLS]])).then_inc(late_in, 16)

            def slot(k, par, a, b, c):
                if a is not None and among(a + 2):
                    load_patches(a + 2, par)
                if a is not None and among(a + 1):
                    load_text(a + 1, 1 - par)
                if c is not None:
                    sp.wait_ge(h2_ready, c + 1)
                    steady(sp)
                    sp.dma_start(tok_d[bass.ds(c * TOK, TOK), :], h2[:]).then_inc(tok_out, 16)
                    sp.wait_ge(hs_ready, c + 1)
                    steady(sp)
                    sp.dma_start(norm_d[bass.ds(c * TOK, TOK), :], hs[:]).then_inc(norm_out, 16)
                    sp.wait_ge(hst_ready, c + 1)
                    steady(sp)
                    sp.dma_start(normt_d[:, :, bass.ds(c * TOK, TOK)], hst[:]).then_inc(normt_out, 16)
                if isinstance(k, int):
                    load_late(k)

            slots(sp, slot)
            sp.wait_ge(tok_out, 16 * IMAGES)
            sp.wait_ge(norm_out, 16 * IMAGES)
            sp.wait_ge(normt_out, 16 * IMAGES)
            sp.wait_ge(late_in, 16 * (len(late) + 2))

        @block.gpsimd
        def _(pool):
            nc.gpsimd.memset(kz[:], 0.0).then_inc(zeroed, 1)
            pool.wait_ge(early_in, EARLY)

            def spread(i, n, var, ready, done, m):
                pool.wait_ge(var, i + 1)
                steady(pool)
                nc.gpsimd.tensor_scalar(ve[:, n:n + 1], m[:, 1:2], 1.0, EPS1, ALU.mult, ALU.add).then_inc(ready, 1)
                pool.wait_ge(ready, i + 1)
                nc.gpsimd.tensor_tensor(rstd[:, n:n + 1], ve[:, n:n + 1], powers[0:TOK, 0:1], ALU.pow).then_inc(done, 1)

            def slot(k, par, a, b, c):
                if a is not None:
                    spread(a, 0, var1, ve1, rstd1, mv)
                if c is not None:
                    spread(c, 1, var2, ve2, rstd2, mv2)
                if a is not None:
                    pool.wait_ge(normed, a + 1)
                    steady(pool)
                    nc.gpsimd.tensor_copy(hkept[:, par, :], h[:, par, :]).then_inc(kept, 1)

            slots(pool, slot)

        @block.scalar
        def _(act):
            act.wait_ge(early_in, EARLY)
            nc.scalar.activation(maskb[:], mask[:], ACT.Copy).then_inc(setup_act, 1)
            nc.scalar.activation(identb[:], ident[:], ACT.Copy).then_inc(setup_act, 1)
            act.wait_ge(setup_vec, 2)
            nc.scalar.activation(pe_row[:], ps[0:EXPERTS, 0, 0:D], ACT.Exp, bias=pstat[:, 0:1],
                                 accum_out=pstat[:, 1:2]).then_inc(setup_act, 1)
            act.wait_ge(setup_pe, 2)
            nc.scalar.activation(pe_col[:], ps[0:HALF, 1, 0:2 * EXPERTS].rearrange("p (c e) -> p c e", c=2),
                                 ACT.Copy).then_inc(setup_act, 1)

            def embedding_out(a, par):
                act.wait_ge(embedded, a + 1)
                if not isinstance(a, int) or a >= 2:
                    act.wait_ge(kept, a - 1)
                    act.wait_ge(normed, a - 1)
                nc.scalar.activation(h[0:PATCHES, par, :], ps[0:PATCHES, EMBED_B, 0:D], ACT.Copy).then_inc(tokens_ready, 1)

            def slot(k, par, a, b, c):
                if c is not None:
                    act.wait_ge(o_turned, c + 1)
                    nc.scalar.activation(ot[0:HALF, :, :], out_view(), ACT.Copy).then_inc(ot_ready, 1)
                if a is not None:
                    act.wait_ge(x_turned, a + 1)
                    nc.scalar.activation(xt[0:HALF, :, :], turn_view(EMBED_B), ACT.Copy).then_inc(xt_ready, 1)
                if b is not None:
                    for hd in range(HEADS):
                        if hd % 4 == 0:
                            act.wait_ge(max_ready, HG * b + hd // 4 + 1)
                        ins = nc.scalar.activation(prob[:, hd, :],
                                                   ps[0:TOK, SCORE_B + hd // 4, (hd % 4) * TOK:(hd % 4 + 1) * TOK],
                                                   ACT.Exp, bias=nmax[:, hd:hd + 1], accum_out=rsum[:, hd:hd + 1])
                        if hd % 4 == 3:
                            ins.then_inc(probs, 1)
                if c is not None:
                    act.wait_ge(hs_turned, c + 1)
                    if later(c):
                        act.wait_ge(normt_out, 16 * c)
                    nc.scalar.activation(hst[:], out_view(), ACT.Copy).then_inc(hst_ready, 1)
                if b is not None:
                    act.wait_ge(probs_turned, 3 * b + 3)
                    nc.scalar.activation(probt[:, 8:12, :], quad_view(2), ACT.Copy).then_inc(turned_act, 1)
                if a is not None:
                    act.wait_ge(v_done, a + 1)
                    if b is not None:
                        act.wait_ge(mixed, b + 1)
                    nc.scalar.activation(v[:], ps[0:TOK, V_B, 0:D], ACT.Copy).then_inc(v_ready, 1)
                    if among(a + 1):
                        embedding_out(a + 1, 1 - par)

            embedding_out(0, 0)
            slots(act, slot)

        @block.vector
        def _(dve):
            nc.vector.memset(fill[:, 0, :], 1.0).then_inc(filled, 1)
            nc.vector.memset(fill[:, 1, :], 0.0).then_inc(filled, 1)
            nc.vector.memset(xt[HALF:128, :, :], 1.0).then_inc(zeroed, 1)
            nc.vector.memset(ot[HALF:128, :, :], 1.0).then_inc(zeroed, 1)
            nc.vector.memset(ones[:], 1.0).then_inc(zeroed, 1)
            dve.wait_ge(early_in, EARLY)
            nc.vector.tensor_tensor(
                wqk[:, :, 0:HG, :].rearrange("p k c (h d) -> p k (c h) d", h=4),
                wqk[:, :, 0:HG, :].rearrange("p k c (h d) -> p k (c h) d", h=4),
                bass.AP(tensor=scl[:].tensor, offset=scl[:].offset,
                        ap=[list(scl[:].ap[0]), [0, 2], [1, HEADS], [0, 32]]), ALU.mult).then_inc(setup_vec, 1)
            dve.wait_ge(setup_pe, 1)
            nc.vector.tensor_reduce(pstat[:, 0:1], ps[0:EXPERTS, 0, 0:D], AX_X, ALU.max, negate=True).then_inc(setup_vec, 1)
            dve.wait_ge(setup_act, 3)
            nc.vector.reciprocal(pstat[:, 2:3], pstat[:, 1:2]).then_inc(setup_vec, 1)
            dve.wait_ge(setup_vec, 3)
            nc.vector.tensor_scalar(pe_row[:], pe_row[:], pstat[:, 2:3], None, ALU.mult).then_inc(setup_vec, 1)

            def stats(i, src, bstats, m, counted, var):
                nc.vector.bn_stats(bstats[:], src).then_inc(counted, 1)
                dve.wait_ge(counted, i + 1)
                steady(dve)
                nc.vector.bn_aggr(m[:], bstats[:]).then_inc(var, 1)

            def norm(i, src, m, done, n, dst, ready):
                dve.wait_ge(done, i + 1)
                nc.vector.tensor_scalar(dst[:], src, m[:, 0:1], rstd[:, n:n + 1], ALU.subtract, ALU.mult).then_inc(ready, 1)

            def slot(k, par, a, b, c):
                if a is not None:
                    dve.wait_ge(tokens_ready, a + 1)
                    dve.wait_ge(text_in[par], loads(a, par))
                    stats(a, h[:, par, :], bst, mv, stats1, var1)
                    norm(a, h[:, par, :], mv, rstd1, 0, xn, normed)
                if b is not None:
                    for q in range(HG):
                        dve.wait_ge(scored, HG * b + q + 1)
                        nc.vector.tensor_reduce(nmax[:, 4 * q:4 * q + 4], quad_view(q), AX_X, ALU.max,
                                                negate=True).then_inc(max_ready, 1)
                if c is not None:
                    dve.wait_ge(projected, c + 1)
                    dve.wait_ge(kept, c + 1)
                    if later(c):
                        dve.wait_ge(tok_out, 16 * c)
                    nc.vector.tensor_tensor(h2[:], ps[0:TOK, OUT_B, 256:256 + D], hkept[:, par, :], ALU.add).then_inc(h2_ready, 1)
                    dve.wait_ge(h2_ready, c + 1)
                    stats(c, h2[:], bst2, mv2, stats2, var2)
                if a is not None:
                    dve.wait_ge(q_done, a + 1)
                    nc.vector.tensor_copy(qt[:], ps[:, Q_B, 0:HG * TOK].rearrange("p (c j) -> p c j", c=HG)).then_inc(q_ready, 1)
                if c is not None:
                    if later(c):
                        dve.wait_ge(norm_out, 16 * c)
                    norm(c, h2[:], mv2, rstd2, 1, hs, hs_ready)
                if b is not None:
                    for c4 in range(2):
                        dve.wait_ge(probs_turned, 3 * b + c4 + 1)
                        nc.vector.tensor_copy(probt[:, 4 * c4:4 * c4 + 4, :], quad_view(c4)).then_inc(turned_vec, 1)
                if a is not None:
                    dve.wait_ge(k_done, a + 1)
                    for j in range(4):
                        ins = nc.vector.tensor_copy(kz[32 * j:32 * j + 32, :, j, :], heads_view(ps[32 * j:32 * j + 32, K_B, 0:HG * TOK]))
                        ins.then_inc(k_ready, 1)
                if b is not None:
                    dve.wait_ge(probs, 3 * b + 3)
                    nc.vector.reciprocal(rinv[:], rsum[:]).then_inc(rinv_ready, 1)
                    dve.wait_ge(rinv_ready, b + 1)
                    dve.wait_ge(mixed, b + 1)
                    nc.vector.tensor_tensor(o[:].rearrange("p (h d) -> p h d", h=HEADS),
                                            ps[0:TOK, SCORE_B, 0:D].rearrange("p (h d) -> p h d", h=HEADS),
                                            bass.AP(tensor=rinv[:].tensor, offset=rinv[:].offset,
                                                    ap=[list(rinv[:].ap[0]), [1, HEADS], [0, DH]]),
                                            ALU.mult).then_inc(o_ready, 1)
                if isinstance(k, int) and k < 2:
                    dve.wait_ge(setup_act, 4)
                    for e in range(EXPERTS // 2 * k, EXPERTS // 2 * (k + 1)):
                        for part in range(2):
                            nc.vector.tensor_scalar(wgate[0:HALF, part, e, :], gatew[0:HALF, part, :], pe_col[:, part, e:e + 1],
                                                    None, ALU.mult).then_inc(setup_vec, 1)

            slots(dve, slot)

        @block.tensor
        def _(pe):
            pe.wait_ge(early_in, EARLY)
            for k in range(2):
                last = nc.tensor.matmul(ps[0:EXPERTS, 0, 0:D], post[0:HALF + k, k, :], wpos[0:HALF + k, k, :],
                                        start=(k == 0), stop=(k == 1))
            last.then_inc(setup_pe, 1)
            pe.wait_ge(setup_vec, 4)
            for k in range(2):
                last = nc.tensor.transpose(ps[0:HALF, 1, EXPERTS * k:EXPERTS * (k + 1)], pe_row[:, HALF * k:HALF * (k + 1)],
                                           ident[0:EXPERTS, 0:EXPERTS])
            last.then_inc(setup_pe, 1)
            pe.wait_ge(setup_act, 4)
            pe.wait_ge(zeroed, 4)

            def turn(src, bank, at):
                for k in range(2):
                    last = nc.tensor.transpose(ps[0:HALF, bank, at + 128 * k:at + 128 * k + TOK], src[:, HALF * k:HALF * (k + 1)],
                                               ident[0:TOK, 0:TOK])
                return last

            def turn_probs(b, c):
                pe.wait_ge(probs, 3 * b + c + 1)
                for j in range(4):
                    last = nc.tensor.transpose(ps[0:TOK, SCORE_B + c, j * TOK:(j + 1) * TOK], prob[:, 4 * c + j, :],
                                               ident[0:TOK, 0:TOK])
                last.then_inc(probs_turned, 1)

            def project_heads(w, bank, done):
                for c in range(HG):
                    for k in range(2):
                        last = nc.tensor.matmul(ps[:, bank, c * TOK:(c + 1) * TOK], wqk[:, k, HG * w + c, :], xt[:, k, :],
                                                start=(k == 0), stop=(k == 1))
                last.then_inc(done, 1)

            def embed(a, par, steps=range(PCH + 1)):
                for ch in steps:
                    if ch == 0:
                        pe.wait_ge(patch_in[par], loads(a, par))
                        if later(a):
                            pe.wait_ge(tokens_ready, a)
                    if ch < PCH:
                        nc.tensor.matmul(ps[0:PATCHES, EMBED_B, 0:D], patch[:, par, ch, :], wpatch[:, ch, :], start=(ch == 0),
                                         stop=False)
                    else:
                        nc.tensor.matmul(ps[0:PATCHES, EMBED_B, 0:D], ones[0:1, 0:PATCHES], bpatch[:], start=False,
                                         stop=True).then_inc(embedded, 1)

            def slot(k, par, a, b, c):
                if c is not None:
                    pe.wait_ge(o_ready, c + 1)
                    if later(c):
                        pe.wait_ge(hst_ready, c)
                    turn(o, OUT_B, 0).then_inc(o_turned, 1)
                if b is not None:
                    if later(b):
                        pe.wait_ge(o_ready, b)
                    for q in range(HG):
                        nc.tensor.matmul(ps[0:TOK, SCORE_B + q, 0:4 * TOK], identb[0:TOK, 0:TOK], maskb[:], start=True, stop=False)
                    pe.wait_ge(q_ready, b + 1)
                    pe.wait_ge(k_ready, 4 * b + 4)
                    for q in range(HG):
                        nc.tensor.matmul(ps[0:TOK, SCORE_B + q, 0:4 * TOK], qt[:, q, :], kz[:, q, :, :], start=False,
                                                stop=True).then_inc(scored, 1)
                if a is not None:
                    pe.wait_ge(normed, a + 1)
                    turn(xn, EMBED_B, 256).then_inc(x_turned, 1)
                if c is not None:
                    pe.wait_ge(ot_ready, c + 1)
                    for k2 in range(2):
                        last = nc.tensor.matmul(ps[0:TOK, OUT_B, 256:256 + D], ot[:, k2, :], wo[:, k2, :], start=(k2 == 0),
                                                stop=(k2 == 1))
                    last.then_inc(projected, 1)
                if a is not None:
                    pe.wait_ge(xt_ready, a + 1)
                    project_heads(0, Q_B, q_done)
                    project_heads(1, K_B, k_done)
                if b is not None:
                    turn_probs(b, 0)
                    turn_probs(b, 1)
                if c is not None:
                    pe.wait_ge(hs_ready, c + 1)
                    turn(hs, OUT_B, 0).then_inc(hs_turned, 1)
                if b is not None:
                    turn_probs(b, 2)
                ahead = a is not None and among(a + 1)
                if ahead:
                    embed(a + 1, 1 - par, range(2) if b is not None else range(PCH + 1))
                if b is not None:
                    pe.wait_ge(turned_act, b + 1)
                    pe.wait_ge(turned_vec, 2 * b + 2)
                    pe.wait_ge(v_ready, b + 1)
                    for hd in range(HEADS):
                        last = nc.tensor.matmul(ps[0:TOK, SCORE_B, hd * DH:(hd + 1) * DH], probt[:, hd, :],
                                                v[:, hd * DH:(hd + 1) * DH], start=True, stop=True)
                        if ahead and hd % 2 and 2 + hd // 2 <= PCH:
                            embed(a + 1, 1 - par, [2 + hd // 2])
                    last.then_inc(mixed, 1)
                if a is not None:
                    if later(a):
                        pe.wait_ge(v_ready, a)
                    for k2 in range(2):
                        last = nc.tensor.matmul(ps[0:TOK, V_B, 0:D], xt[:, k2, :], wv[:, k2, :], start=(k2 == 0), stop=(k2 == 1))
                    last.then_inc(v_done, 1)

            embed(0, 0)
            slots(pe, slot)


FINAL_ACT = {1: 0, 3: 1, 6: 2, 9: 3, 14: 4}
FINAL_PE = {5: 0, 8: 1, 13: 2}
FINAL_POOL = {0: 0, 2: 1, 10: 2, 15: 3}
TURN = 2
DOWN_LAG = 3
PREPARE = 8
REST_LIST = [(0, None, 0), (1, None, 1), (2, "band", 0), (3, "band", 1)]
assert len(REST_LIST) == REST_UNITS

MISC_B, LOOK_B, XG_B, GU_B, Y_B, CODE_B = 0, 1, 3, 4, 5, 6


def units_of(m):
    first = [(0, None, 0), (1, None, 1)] if m == 0 else []
    return first + [(2 + GRP * m + j, GRP * m + j, None) for j in range(GRP)]


def unit_spots(m):
    n = len(units_of(m))
    return [3 + 3 * j for j in range(n)] if n == 4 else [2 + 2 * j for j in range(n)]


def gate_spots():
    return {3: (0, 0), 6: (0, 1), 11: (1, 0), 14: (1, 1)}


def experts(nc, sb, sem, tok_d, norm_d, normt_d, digit_d, out, ident, wgate, gatew, pe_col, rows, table, wshared, wsdown, wexp, wdown,
            wm1, wm2, colv, place, powers, codef, ps):
    keys = sb("keys", [TILE, BPT, GRP, D])
    keys_rest = sb("keys_rest", [TILE, BANDS, D])
    vals = sb("vals", [TILE, 2, GRP, TOP])
    idx = sb("idx", [TILE, 2, GRP, TOP], U16)
    digits = sb("digits", [TILE, 2, 2, COLS], U16)
    dcode = sb("dcode", [TILE, 2, 2, 2, COLS], BF16)
    codew = sb("codew", [128, 2, 128], BF16)
    code = sb("code", [TILE, 4, 2, COLS], BF16)
    ntop = sb("ntop", [TILE, 2, GRP])
    esum = sb("esum", [TILE, 2, GRP])
    einv = sb("einv", [TILE, 2, GRP])
    ew = sb("ew", [TILE, 2, GRP, TOP])
    looked_s = sb("looked_s", [TILE, 4, COLS])
    picked = sb("picked", [TILE, 4, COLS])
    xs = sb("xs", [TILE, GRP, TOP])
    xw = sb("xw", [TILE, GRP, TOP])
    xwt = sb("xwt", [TOP, GRP, TILE])
    gu_s = sb("gu_s", [HALF, 2, 2, 2, TILE])
    tanh_s = sb("tanh_s", [HALF, 2, 2, TILE])
    prod_s = sb("prod_s", [HALF, 2, 2, TILE])
    turned_s = sb("turned_s", [HALF, 2, 2, TILE])
    hid = sb("hid", [HALF, 2, 2, TILE])
    nt_gate = sb("nt_gate", [HALF + 1, 2, TILE])
    nt_mlp = sb("nt_mlp", [HALF, 2, TILE])
    nt_rest = sb("nt_rest", [HALF, 2, REST])
    nt_packed = sb("nt_packed", [HALF + 1, 2, BANDS, PACK, REST])
    hr = sb("hr", [HALF, OCT, LO])
    rest = sb("rest", [HALF, OCT, LO])
    parts = sb("parts", [HALF, OCT, 3, LO], BF16)
    resid = sb("resid", [TILE, D])
    y = sb("y", [TILE, D])
    ysq = sb("ysq", [TILE, D])
    yn = sb("yn", [TILE, D])
    st = sb("st", [TILE, 6])
    zt = sb("zt", [HALF, 2, TILE])
    st1 = sb("st1", [HALF + 1, 2, TILE])
    m2s = sb("m2s", [TILE, D])
    fin = sb("fin", [TILE, D])

    nt_gate_in, nt_mlp_in, hr_in, resid_in = sem("nt_gate_in"), sem("nt_mlp_in"), sem("hr_in"), sem("resid_in")
    b_ones, b_codew = sem("b_ones"), sem("b_codew")
    gated, keys_ready = sem("gated"), sem("keys_ready")
    chains = sem("chain_first"), sem("chain_second")
    plain = sem("plain")
    ranked, coded, digits_out, rows_in = sem("ranked"), sem("coded"), sem("digits_out"), sem("rows_in")
    inverted = sem("inverted")
    weights_ready = sem("weights_ready")
    code_done, code_ready = sem("code_done"), sem("code_ready")
    rounded = sem("rounded")
    split, table_in = sem("split"), (sem("table_first_in"), sem("table_second_in"))
    looked, looked_out, picked_ready, placed = sem("looked"), sem("looked_out"), sem("picked_ready"), sem("placed")
    scaled, weighted, x_turned, xwt_ready = sem("scaled"), sem("weighted"), sem("x_turned"), sem("xwt_ready")
    gate_up, activated, half_hidden = sem("gate_up"), sem("activated"), sem("half_hidden")
    hidden, downed, biased = sem("hidden"), sem("downed"), sem("biased")
    y_out, mean_ready, squared, var_ready, rstd_ready = (sem("y_out"), sem("mean_ready"), sem("squared"),
                                                         sem("var_ready"), sem("rstd_ready"))
    shift_ready, yn_ready, y_turned, zt_ready = sem("shift_ready"), sem("yn_ready"), sem("y_turned"), sem("zt_ready")
    tanh_ready, half_st1 = sem("tanh_ready"), sem("half_st1")
    m1_done, st1_ready, m2_done, m2_out, fin_ready = (sem("m1_done"), sem("st1_ready"), sem("m2_done"),
                                                      sem("m2_out"), sem("fin_ready"))
    out_done = sem("out_done")
    nt_rest_in, packed = sem("nt_rest_in"), sem("packed")
    passed = sem("passed")
    TABLE = 16 * PER

    def steady(eng):
        eng.sem_inc(passed, 1)

    def slots(eng, slot):
        slot(0, 0, False)
        for g in range(3):
            slot(1, g, True)
        with eng.Fori(1, TILES - 1) as t:
            slot(t, 3, True)
            for g in range(3):
                slot(t + 1, g, True)
        slot(TILES - 1, 3, True)
        for g in range(BPT):
            slot(TILES, g, True)

    def is_rest(t):
        return isinstance(t, int) and t == 0

    def last_tile(t):
        return isinstance(t, int) and t == TILES

    def last_block(n):
        return isinstance(n, int) and n == BPT * TILES

    def parity(t, g):
        return 0 if is_rest(t) else (g + 1) % 2

    def block_no(t, g):
        return 0 if is_rest(t) else BPT * (t - 1) + g + 1

    def units_before(t):
        return 0 if is_rest(t) else REST_UNITS + UNITS * (t - 1)

    def pairs_before(t, g):
        return 0 if is_rest(t) else BANDS // 2 + 2 * (BPT * (t - 1) + g)

    def experts_of(n):
        return BANDS if isinstance(n, int) and n == 0 else GRP

    def start(t):
        return TILES * TILE if is_rest(t) else (t - 1) * TILE

    def mlps(t, g):
        m = (g - 1) % BPT
        tm = t if g else t - 1
        if is_rest(tm):
            return tm, REST_LIST, unit_spots(3)
        return tm, units_of(m), unit_spots(m)

    def gates_of(t, g):
        if is_rest(t):
            return {o: (2 + b, pair) for o, (b, pair) in gate_spots().items()}
        if g % 2 == 0 or last_tile(t):
            return {}
        return {o: (g - 1 + b, pair) for o, (b, pair) in gate_spots().items()}

    def gated_before(t, g):
        return pairs_before(t + 1, 0) + (4 if g in (2, 3) and not last_tile(t) else 0)

    with nc.Block() as block:

        @block.sync
        def _(sp):
            def load_tokens(t):
                for j in range(PER):
                    first = start(t) + (0 if is_rest(t) else j * OCT)
                    sp.dma_start(hr[HI * j:HI * (j + 1), :, :],
                                 norm_d[bass.ds(first, OCT), :].rearrange("o (hi lo) -> hi o lo", lo=LO)).then_inc(hr_in, 16)

            def load_gate(t):
                sp.dma_start(nt_gate[0:HALF, :, :], normt_d[:, :, bass.ds(start(t), TILE)]).then_inc(nt_gate_in, 16)

            def load_mlp(t):
                sp.dma_start(nt_mlp[:], normt_d[:, :, bass.ds(start(t), TILE)]).then_inc(nt_mlp_in, 16)

            def build_table(t, part):
                sp.wait_ge(split, t + 1)
                if not is_rest(t):
                    sp.wait_ge(looked, OCT * block_no(t, 0) - OCT // 2 * (1 - part))
                steady(sp)
                octs = slice(OCT // 2 * part, OCT // 2 * (part + 1))
                for j in range(PER):
                    sp.dma_start(table[HI * j:HI * (j + 1), octs, :, LO * j:LO * (j + 1)].rearrange("p o s l -> p (o s) l"),
                                 parts[HI * j:HI * (j + 1), octs].rearrange("p o s l -> p (o s) l")).then_inc(table_in[part], 16)

            sp.dma_start(nt_rest[:], normt_d[:, :, TILES * TILE:TOKENS]).then_inc(nt_rest_in, 16)
            load_tokens(0)
            load_gate(1)
            load_mlp(1)
            sp.dma_start(resid[0:REST, :], tok_d[TILES * TILE:TOKENS, :]).then_inc(resid_in, 16)
            sp.wait_ge(b_ones, 4)
            build_table(0, 0)
            build_table(0, 1)
            load_tokens(1)

            def slot(t, g, mlp):
                n, par = block_no(t, g), parity(t, g)
                if g == 1 and not last_tile(t):
                    sp.wait_ge(gated, pairs_before(t + 1, 0))
                    steady(sp)
                    sp.wait_ge(split, t + 1)
                    steady(sp)
                    load_gate(t + 1)
                    load_tokens(t + 1)
                sp.wait_ge(coded, n + 1)
                steady(sp)
                w = experts_of(n) * TOP
                sp.dma_start(digit_d[par].rearrange("a k p c -> p (a k) c")[:, :, 0:w],
                             dcode[:, par].rearrange("p a k c -> p (a k) c")[:, :, 0:w]).then_inc(digits_out, 16)
                sp.wait_ge(digits_out, 16 * n + 16)
                steady(sp)
                if not isinstance(n, int) or n >= 2:
                    sp.wait_ge(code_done, OCT * n - OCT)
                    steady(sp)
                for a in range(2):
                    sp.dma_start(rows[LOW_P * a:LOW_P * a + 2 * PER, par, :, 0:w],
                                 digit_d[par, a].rearrange("k (t o) c -> (k t) o c", o=OCT)[:, :, 0:w]).then_inc(rows_in, 16)
                if is_rest(t):
                    build_table(1, 0)
                elif g == 0:
                    build_table(t, 1)
                if g == 2 and not last_tile(t):
                    sp.wait_ge(gate_up, units_before(t) + 2)
                    steady(sp)
                    load_mlp(t + 1)
                if g == 3:
                    sp.wait_ge(fin_ready, t)
                    steady(sp)
                    sp.dma_start(resid[:], tok_d[bass.ds(start(t), TILE), :]).then_inc(resid_in, 16)
                    if not last_tile(t):
                        build_table(t + 1, 0)

            slots(sp, slot)
            sp.wait_ge(out_done, 16 * TILES + 16)

        @block.vector
        def _(dve):
            nc.vector.memset(nt_gate[HALF:HALF + 1, :, :], 1.0).then_inc(b_ones, 1)
            nc.vector.memset(st1[HALF:HALF + 1, :, :], 2.0).then_inc(b_ones, 1)
            nc.vector.memset(nt_packed[HALF:HALF + 1], 1.0).then_inc(b_ones, 1)
            nc.vector.memset(ps[:, Y_B, 0:D], 0.0).then_inc(b_ones, 1)

            LAST_STEP = 2 * (2 * ROUNDS - 1) + 1

            def close_pair(pair):
                dve.wait_ge(chains[pair], LAST_STEP)
                dve.sem_clear(chains[pair])

            def close_block(n, par):
                many = experts_of(n)
                last = 1 if many > 2 else 0
                dve.wait_ge(chains[last], LAST_STEP)
                nc.vector.tensor_scalar(ntop[:, par, 0:many], vals[:, par, 0:many, 0], -1.0, None, ALU.mult)
                if not (isinstance(n, int) and n < 2):
                    dve.wait_ge(plain, n - 1)
                src = idx[:, par, 0:many].rearrange("p e r -> p (e r)")
                nc.vector.tensor_scalar(digits[:, par, 0, 0:many * TOP], src, 4, None, ALU.logical_shift_right)
                nc.vector.tensor_scalar(digits[:, par, 1, 0:many * TOP], src, LO - 1, None, ALU.bitwise_and).then_inc(ranked, 1)
                dve.sem_clear(chains[last])

            def slot(t, g, mlp):
                n, par = block_no(t, g), parity(t, g)
                many = experts_of(n)
                from_keys = keys_rest if is_rest(t) else keys[:, g]
                for pair in range(many // 2):
                    chain = chains[pair]
                    dve.wait_ge(keys_ready, pairs_before(t, g) + pair + 1)
                    if pair == 0 and not (isinstance(n, int) and n < 2):
                        dve.wait_ge(weights_ready, n - 1)
                    steady(dve)
                    done = 0
                    two = [2 * pair, 2 * pair + 1]
                    for r in range(ROUNDS):
                        at = slice(8 * r, 8 * r + 8)
                        for x, e in enumerate(two):
                            if r:
                                dve.wait_ge(chain, done - 1 + x)
                            nc.vector.max(vals[:, par, e, at], from_keys[:, e, :]).then_inc(chain, 1)
                        done += 2
                        for x, e in enumerate(two):
                            dve.wait_ge(chain, done - 1 + x)
                            found = nc.vector.max_index(idx[:, par, e, at], vals[:, par, e, at], from_keys[:, e, :])
                            if r < ROUNDS - 1:
                                nc.vector.match_replace(from_keys[:, e, :], vals[:, par, e, at], from_keys[:, e, :],
                                                        NEG).then_inc(chain, 1)
                        if r < ROUNDS - 1:
                            done += 2
                        if r == 0 and pair:
                            close_pair(0)
                        if r == 0 and pair == 0 and not (isinstance(n, int) and n < 2):
                            close_block(n - 1, 1 - par)
                    found.then_inc(chain, 1)
                    done += 1
                    assert done == LAST_STEP
                if last_block(n) or is_rest(t):
                    close_block(n, par)

            slots(dve, slot)

        @block.scalar
        def _(act):
            def keys_out(t, g, pair):
                act.wait_ge(gated, pairs_before(t, g) + pair + 1)
                nc.scalar.activation(keys_rest[:] if is_rest(t) else keys[:, g, 2 * pair:2 * pair + 2, :],
                                     ps[:, MISC_B, 0:2 * D].rearrange("p (e f) -> p e f", e=2),
                                     ACT.Copy).then_inc(keys_ready, 1)

            def turned_out(n):
                many = experts_of(n)
                act.wait_ge(x_turned, n + 1)
                nc.scalar.activation(xwt[:, 0:many], ps[0:TOP, MISC_B, 0:many * TILE].rearrange("p (e j) -> p e j", e=many),
                                     ACT.Copy).then_inc(xwt_ready, 1)

            def prepare(n, par):
                act.wait_ge(ranked, n + 1)
                if not isinstance(n, int) or n >= 2:
                    act.wait_ge(digits_out, 16 * n - 16)
                w = experts_of(n) * TOP
                nc.scalar.activation(dcode[:, par, :, 1, 0:w], digits[:, par, :, 0:w], ACT.Copy).then_inc(plain, 1)

            def exponentials(n, par, e):
                if e == 0 and (not isinstance(n, int) or n >= 2):
                    act.wait_ge(weighted, n - 1)
                ins = nc.scalar.activation(ew[:, par, e, :], vals[:, par, e, :], ACT.Exp, bias=ntop[:, par, e:e + 1],
                                           accum_out=esum[:, par, e:e + 1])
                if e == experts_of(n) - 1:
                    ins.then_inc(weights_ready, 1)

            def code_out(n, o, first):
                act.wait_ge(code_done, OCT * n + o + 1)
                if not first or o >= 4:
                    act.wait_ge(picked_ready, OCT * n + o - 3)
                w = experts_of(n) * TOP
                nc.scalar.activation(code[:, o % 4, :, 0:w], ps[:, CODE_B:CODE_B + 2, 0:w], ACT.Relu).then_inc(code_ready, 1)

            def slot(t, g, mlp):
                n, par = block_no(t, g), parity(t, g)
                tm, units, spots = mlps(t, g) if mlp else (None, [], [])
                gates = gates_of(t, g)
                for o in range(OCT):
                    act.wait_ge(looked, OCT * n + o + 1)
                    if mlp or o >= 4:
                        act.wait_ge(picked_ready, OCT * n + o - 3)
                    w = experts_of(n) * TOP
                    nc.scalar.activation(looked_s[:, o % 4, 0:w], ps[:, LOOK_B + o % 2, 0:w], ACT.Copy).then_inc(looked_out, 1)
                    if o + 2 < OCT:
                        code_out(n, o + 2, not mlp)
                    if o == TURN and mlp:
                        turned_out(n - 1)
                    if o == PREPARE and not last_block(n):
                        prepare(n + 1, 1 - par)
                    if o > PREPARE and o - PREPARE <= GRP and not last_block(n):
                        exponentials(n + 1, 1 - par, o - PREPARE - 1)
                    if o in gates:
                        keys_out(t + 1, *gates[o])
                    for (u, e, half), spot in zip(units, spots):
                        if spot == o:
                            activate(tm, u, e)
                    if g == 2 and o in FINAL_ACT:
                        final(t - 1, FINAL_ACT[o])
                if not last_block(n):
                    code_out(n + 1, 0, False)
                    code_out(n + 1, 1, False)
                scale_out(n, par)
                if mlp and g == 0:
                    y_taken(tm)

            def activate(tm, u, e):
                width = REST if is_rest(tm) and e is None else TILE
                act.wait_ge(gate_up, units_before(tm) + u + 1)
                if u >= 2 or not is_rest(tm):
                    act.wait_ge(hidden, units_before(tm) + u - 1)
                gu = ps[0:HALF, GU_B, :].rearrange("p (a c j) -> p a c j", a=2, c=2)
                if width == TILE:
                    nc.scalar.activation(tanh_s[:, u % 2], gu[:, 0], ACT.Tanh, scale=0.5)
                    nc.scalar.activation(gu_s[:, u % 2], gu, ACT.Copy).then_inc(activated, 1)
                else:
                    nc.scalar.activation(tanh_s[:, u % 2, :, 0:width], gu[:, 0, :, 0:width], ACT.Tanh, scale=0.5)
                    for a in range(2):
                        ins = nc.scalar.activation(gu_s[:, u % 2, a, :, 0:width], gu[:, a, :, 0:width], ACT.Copy)
                    ins.then_inc(activated, 1)

            def scale_out(n, par):
                act.wait_ge(placed, OCT * n + OCT)
                act.wait_ge(inverted, n + 1)
                if not isinstance(n, int) or n >= 1:
                    act.wait_ge(weighted, n)
                for e in range(experts_of(n)):
                    ins = nc.scalar.activation(xs[:, e, :], ps[:, XG_B, e * TOP:(e + 1) * TOP], ACT.Copy,
                                               scale=einv[:, par, e:e + 1])
                ins.then_inc(scaled, 1)

            def y_taken(t):
                act.wait_ge(downed, units_before(t + 1))
                if not (isinstance(t, int) and t == 0):
                    act.wait_ge(yn_ready, t)
                nc.scalar.activation(y[:], ps[:, Y_B, 0:D], ACT.Copy, scale=0.5, accum_out=st[:, 0:1]).then_inc(y_out, 1)

            def final(t, step):
                if step == 0:
                    act.wait_ge(mean_ready, t + 1)
                    nc.scalar.activation(ysq[:], y[:], ACT.Square, bias=st[:, 1:2], accum_out=st[:, 2:3]).then_inc(squared, 1)
                if step == 1:
                    act.wait_ge(shift_ready, t + 1)
                    nc.scalar.activation(yn[:], y[:], ACT.Identity, scale=st[:, 4:5], bias=st[:, 5:6]).then_inc(yn_ready, 1)
                if step == 2:
                    act.wait_ge(y_turned, t + 1)
                    for k in range(2):
                        ins = nc.scalar.activation(zt[:, k, :], ps[0:HALF, MISC_B, k * TILE:(k + 1) * TILE], ACT.Identity,
                                                   scale=colv[:, 2 + k:3 + k], bias=colv[:, 4 + k:5 + k])
                    ins.then_inc(zt_ready, 1)
                if step == 3:
                    act.wait_ge(m1_done, t + 1)
                    for k in range(2):
                        ins = nc.scalar.activation(st1[0:HALF, k, :], ps[0:HALF, MISC_B, (2 + k) * TILE:(3 + k) * TILE],
                                                   ACT.Identity, bias=colv[:, k:k + 1])
                    ins.then_inc(biased, 1)
                    act.wait_ge(biased, t + 1)
                    steady(act)
                    nc.scalar.activation(zt[:], st1[0:HALF], ACT.Tanh, scale=0.5).then_inc(tanh_ready, 1)
                if step == 4:
                    act.wait_ge(m2_done, t + 1)
                    if not (isinstance(t, int) and t == 0):
                        act.wait_ge(fin_ready, t)
                    nc.scalar.activation(m2s[:], ps[:, MISC_B, 0:D], ACT.Copy, scale=0.5).then_inc(m2_out, 1)

            nc.scalar.activation(codew[:], codef[:], ACT.Copy).then_inc(b_codew, 1)
            keys_out(0, 0, 0)
            for g in range(2):
                for pair in range(2):
                    keys_out(1, g, pair)
            prepare(0, 0)
            for e in range(BANDS):
                exponentials(0, 0, e)
            code_out(0, 0, True)
            code_out(0, 1, True)
            slots(act, slot)
            turned_out(BPT * TILES)
            for u, e, half in units_of(BPT - 1):
                activate(TILES, u, e)
            y_taken(TILES)
            for step in range(5):
                final(TILES, step)

        @block.gpsimd
        def _(pool):
            def split_part(t, step):
                if step == 0:
                    pool.wait_ge(hr_in, 16 * PER * t + 16 * PER)
                    if not (isinstance(t, int) and t == 0):
                        for half_in in table_in:
                            pool.wait_ge(half_in, TABLE * t)
                    steady(pool)
                    nc.gpsimd.tensor_copy(parts[:, :, 0, :], hr[:]).then_inc(rounded, 1)
                if step == 1:
                    pool.wait_ge(rounded, 3 * t + 1)
                    nc.gpsimd.tensor_tensor(rest[:], hr[:], parts[:, :, 0, :], ALU.subtract).then_inc(rounded, 1)
                if step == 2:
                    pool.wait_ge(rounded, 3 * t + 2)
                    steady(pool)
                    nc.gpsimd.tensor_copy(parts[:, :, 1, :], rest[:]).then_inc(rounded, 1)
                if step == 3:
                    pool.wait_ge(rounded, 3 * t + 3)
                    nc.gpsimd.tensor_tensor(parts[:, :, 2, :], rest[:], parts[:, :, 1, :], ALU.subtract).then_inc(split, 1)

            def hide(tm, u, e):
                width = REST if is_rest(tm) and e is None else TILE
                before = units_before(tm) + u
                pool.wait_ge(activated, before + 1)
                if u >= 2 or not is_rest(tm):
                    pool.wait_ge(downed, before - 1)
                w = slice(0, width)
                nc.gpsimd.tensor_tensor(prod_s[:, u % 2, :, w], gu_s[:, u % 2, 0, :, w], gu_s[:, u % 2, 1, :, w], ALU.mult).then_inc(half_hidden, 1)
                pool.wait_ge(half_hidden, 2 * before + 1)
                nc.gpsimd.tensor_tensor(turned_s[:, u % 2, :, w], prod_s[:, u % 2, :, w], tanh_s[:, u % 2, :, w], ALU.mult).then_inc(half_hidden, 1)
                pool.wait_ge(half_hidden, 2 * before + 2)
                nc.gpsimd.tensor_tensor(hid[:, u % 2, :, w], prod_s[:, u % 2, :, w], turned_s[:, u % 2, :, w], ALU.add).then_inc(hidden, 1)

            def pack():
                pool.wait_ge(nt_rest_in, 16)
                for k in range(2):
                    t_ap, p_ap = nt_rest[:, k, :], pe_col[:, k, :]
                    nc.gpsimd.tensor_tensor(
                        nt_packed[0:HALF, k].rearrange("p b e j -> p (b e) j"),
                        bass.AP(tensor=t_ap.tensor, offset=t_ap.offset, ap=[list(t_ap.ap[0]), [0, EXPERTS], [1, REST]]),
                        bass.AP(tensor=p_ap.tensor, offset=p_ap.offset, ap=[list(p_ap.ap[0]), [1, EXPERTS], [0, REST]]),
                        ALU.mult).then_inc(packed, 1)

            def square(n, par):
                pool.wait_ge(plain, n + 1)
                w = slice(0, experts_of(n) * TOP)
                nc.gpsimd.tensor_tensor(dcode[:, par, :, 0, w], dcode[:, par, :, 1, w], dcode[:, par, :, 1, w],
                                        ALU.mult).then_inc(coded, 1)

            def slot(t, g, mlp):
                n, par = block_no(t, g), parity(t, g)
                tm, units, spots = mlps(t, g) if mlp else (None, [], [])
                pool.wait_ge(weights_ready, n + 1)
                many = experts_of(n)
                nc.gpsimd.tensor_tensor(einv[:, par, 0:many], esum[:, par, 0:many], powers[:, 4:4 + many], ALU.pow).then_inc(inverted, 1)
                for o in range(OCT):
                    pool.wait_ge(looked_out, OCT * n + o + 1)
                    if mlp or o >= 4:
                        pool.wait_ge(placed, OCT * n + o - 3)
                    w = slice(0, experts_of(n) * TOP)
                    nc.gpsimd.tensor_tensor(picked[:, o % 4, w], looked_s[:, o % 4, w], code[:, o % 4, 1, w],
                                            ALU.mult).then_inc(picked_ready, 1)
                    if o == PREPARE and not last_block(n):
                        square(n + 1, 1 - par)
                    for (u, e, half), spot in zip(units, spots):
                        if spot == o:
                            hide(tm, u, e)
                    if (g == 3 and not last_tile(t) or is_rest(t)) and o in (1, 3, 5, 7):
                        split_part(t + 1, o // 2)
                    if g == 2 and o in FINAL_POOL:
                        final(t - 1, FINAL_POOL[o])
                pool.wait_ge(scaled, n + 1)
                if mlp:
                    pool.wait_ge(x_turned, n)
                e = slice(0, experts_of(n))
                nc.gpsimd.tensor_tensor(xw[:, e], xs[:, e], ew[:, par, e], ALU.mult).then_inc(weighted, 1)

            def final(t, step):
                if step == 0:
                    pool.wait_ge(y_out, t + 1)
                    steady(pool)
                    nc.gpsimd.tensor_scalar(st[:, 1:2], st[:, 0:1], -1.0 / D, 0.0, ALU.mult, ALU.add).then_inc(mean_ready, 1)
                if step == 1:
                    pool.wait_ge(squared, t + 1)
                    steady(pool)
                    nc.gpsimd.tensor_scalar(st[:, 3:4], st[:, 2:3], 1.0 / D, EPS2, ALU.mult, ALU.add).then_inc(var_ready, 1)
                    pool.wait_ge(var_ready, t + 1)
                    nc.gpsimd.tensor_tensor(st[:, 4:5], st[:, 3:4], powers[:, 0:1], ALU.pow).then_inc(rstd_ready, 1)
                    pool.wait_ge(rstd_ready, t + 1)
                    nc.gpsimd.tensor_tensor(st[:, 5:6], st[:, 1:2], st[:, 4:5], ALU.mult).then_inc(shift_ready, 1)
                if step == 2:
                    pool.wait_ge(tanh_ready, t + 1)
                    nc.gpsimd.tensor_tensor(zt[:], zt[:], st1[0:HALF], ALU.mult).then_inc(half_st1, 1)
                    pool.wait_ge(half_st1, t + 1)
                    nc.gpsimd.tensor_tensor(st1[0:HALF], zt[:], st1[0:HALF], ALU.add).then_inc(st1_ready, 1)
                if step == 3:
                    pool.wait_ge(m2_out, t + 1)
                    pool.wait_ge(resid_in, 16 * t + 16)
                    if not (isinstance(t, int) and t == 0):
                        pool.wait_ge(out_done, 16 * t)
                    r = slice(0, REST if is_rest(t) else TILE)
                    nc.gpsimd.tensor_tensor(fin[r], m2s[r], resid[r], ALU.add).then_inc(fin_ready, 1)
                    pool.wait_ge(fin_ready, t + 1)
                    rows_out = REST if is_rest(t) else TILE
                    pool.dma_start(out[bass.ds(start(t), rows_out), :], fin[0:rows_out, :]).then_inc(out_done, 16)

            pack()
            for step in range(4):
                split_part(0, step)
            square(0, 0)
            slots(pool, slot)
            for u, e, half in units_of(BPT - 1):
                hide(TILES, u, e)
            for step in range(4):
                final(TILES, step)

        @block.tensor
        def _(pe):
            def gate(t, g, pair):
                pe.wait_ge(keys_ready, pairs_before(t, g) + pair)
                for k in range(2):
                    ins = nc.tensor.matmul(ps[:, MISC_B, 0:2 * D], nt_gate[0:HALF + k, k, :],
                                           wgate[0:HALF + k, k, GRP * g + 2 * pair:GRP * g + 2 * pair + 2, :],
                                           start=(k == 0), stop=(k == 1))
                ins.then_inc(gated, 1)

            def gate_rest():
                pe.wait_ge(packed, 2)
                for band in range(BANDS):
                    for k in range(2):
                        ins = nc.tensor.matmul(ps[:, MISC_B, band * D:(band + 1) * D], nt_packed[0:HALF + k, k, band],
                                               gatew[0:HALF + k, k, :], start=(k == 0), stop=(k == 1))
                ins.then_inc(gated, 1)

            def make_code(n, par, o, first):
                if not (first and o == 0):
                    pe.wait_ge(code_ready, OCT * n + o)
                w = slice(0, experts_of(n) * TOP)
                for a in range(2):
                    ins = nc.tensor.matmul(ps[:, CODE_B + a, w], codew[:, a, :], rows[:, par, o, w],
                                           start=True, stop=True)
                ins.then_inc(code_done, 1)

            def first_codes(n, par, o):
                if o == 0:
                    pe.wait_ge(rows_in, 32 * n + 32)
                make_code(n, par, o, isinstance(n, int) and n == 0)

            def look(n, o, first):
                w = slice(0, experts_of(n) * TOP)
                pe.wait_ge(code_ready, OCT * n + o + 1)
                if not (first and o < 2):
                    pe.wait_ge(looked_out, OCT * n + o - 1)
                for s in range(3):
                    ins = nc.tensor.matmul(ps[:, LOOK_B + o % 2, w], table[:, o, s, :], code[:, o % 4, 0, w],
                                           start=(s == 0), stop=(s == 2))
                ins.then_inc(looked, 1)

            def put(n, o, first):
                if o == 0 and not first:
                    pe.wait_ge(scaled, n)
                pe.wait_ge(picked_ready, OCT * n + o + 1)
                w = slice(0, experts_of(n) * TOP)
                nc.tensor.matmul(ps[:, XG_B, w], place[:, OCT - 1 - o:OCT - 1 - o + TILE], picked[:, o % 4, w],
                                 start=(o == 0), stop=(o == OCT - 1)).then_inc(placed, 1)

            def turn_x(n, t, g):
                pe.wait_ge(keys_ready, gated_before(t, g))
                if g == 3:
                    pe.wait_ge(m2_out, t)
                pe.wait_ge(weighted, n + 1)
                for e in range(experts_of(n)):
                    ins = nc.tensor.transpose(ps[0:TOP, MISC_B, e * TILE:(e + 1) * TILE], xw[:, e, :], ident[:])
                ins.then_inc(x_turned, 1)

            def up(tm, u, e, half):
                rest = is_rest(tm)
                if e is None and half == 0 and not rest:
                    pe.wait_ge(nt_mlp_in, 16 * tm)
                if e == "band":
                    pe.wait_ge(xwt_ready, 1)
                elif e is not None and (e % GRP == 0):
                    pe.wait_ge(xwt_ready, block_no(tm, e // GRP) + 1)
                if u or not rest:
                    pe.wait_ge(activated, units_before(tm) + u)
                for a in range(2):
                    for c in range(2):
                        wide = REST if rest and e is None else TILE
                        dst = ps[0:HALF, GU_B, (2 * a + c) * TILE:(2 * a + c) * TILE + wide]
                        if e is None:
                            for k in range(2):
                                ins = nc.tensor.matmul(dst, wshared[:, k, 2 * a + half, c * HALF:(c + 1) * HALF],
                                                       (nt_rest if rest else nt_mlp)[:, k, :], start=(k == 0), stop=(k == 1))
                        elif e == "band":
                            for x in range(PACK):
                                own = slice(x * REST, (x + 1) * REST)
                                ins = nc.tensor.matmul(dst[:, own],
                                                       wexp[:, half * PACK + x, a * D + c * HALF:a * D + (c + 1) * HALF],
                                                       xwt[:, half, own], start=True, stop=True)
                        else:
                            at = a * D + c * HALF
                            ins = nc.tensor.matmul(dst, wexp[:, e, at:at + HALF], xwt[:, e % GRP, :], start=True, stop=True)
                ins.then_inc(gate_up, 1)

            def down(tm, u, e, half):
                rest = is_rest(tm)
                if u == 0 and not rest:
                    pe.wait_ge(y_out, tm)
                pe.wait_ge(hidden, units_before(tm) + u + 1)
                last_u = (REST_UNITS if rest else UNITS) - 1
                many = PACK if e == "band" else 1
                for x in range(many):
                    for c in range(2):
                        if e is None:
                            w = wsdown[:, 2 * half + c, :]
                        else:
                            w = wdown[:, half * PACK + x if rest else e, c, :]
                        own = slice(x * REST, (x + 1) * REST) if rest else slice(0, TILE)
                        ins = nc.tensor.matmul(ps[0:REST if rest else TILE, Y_B, 0:D], hid[:, u % 2, c, own], w,
                                               start=(u == 0 and c == 0), stop=(u == last_u and x == many - 1 and c == 1))
                ins.then_inc(downed, 1)

            def final(t, step):
                if step == 0:
                    pe.wait_ge(yn_ready, t + 1)
                    for k in range(2):
                        ins = nc.tensor.transpose(ps[0:HALF, MISC_B, k * TILE:(k + 1) * TILE], yn[:, k * HALF:(k + 1) * HALF], ident[:])
                    ins.then_inc(y_turned, 1)
                if step == 1:
                    pe.wait_ge(zt_ready, t + 1)
                    for c in range(2):
                        for k in range(2):
                            ins = nc.tensor.matmul(ps[0:HALF, MISC_B, (2 + c) * TILE:(3 + c) * TILE],
                                                   wm1[:, k, c * HALF:(c + 1) * HALF], zt[:, k, :], start=(k == 0), stop=(k == 1))
                    ins.then_inc(m1_done, 1)
                if step == 2:
                    pe.wait_ge(st1_ready, t + 1)
                    for k in range(2):
                        ins = nc.tensor.matmul(ps[:, MISC_B, 0:D], st1[0:HALF + k, k, :], wm2[0:HALF + k, k, :],
                                               start=(k == 0), stop=(k == 1))
                    ins.then_inc(m2_done, 1)

            def slot(t, g, mlp):
                n, par = block_no(t, g), parity(t, g)
                tm, units, spots = mlps(t, g) if mlp else (None, [], [])
                gates = gates_of(t, g)
                if g == 1 and not last_tile(t):
                    pe.wait_ge(nt_gate_in, 16 * (t + 1))
                for o in range(OCT):
                    if g == 0 and o in (0, OCT // 2):
                        pe.wait_ge(table_in[1 if o else 0], TABLE * t + TABLE)
                    look(n, o, not mlp)
                    if o == TURN and mlp:
                        turn_x(n - 1, t, g)
                    if o + 2 < OCT:
                        make_code(n, par, o + 2, False)
                    if o >= 3:
                        put(n, o - 3, not mlp)
                    if o in gates:
                        gb, pair = gates[o]
                        if gb == g - 1 and pair == 0 and mlp:
                            pe.wait_ge(xwt_ready, n)
                        gate(t + 1, gb, pair)
                    for (u, e, half), spot in zip(units, spots):
                        if spot == o:
                            up(tm, u, e, half)
                        if spot + DOWN_LAG == o:
                            down(tm, u, e, half)
                    if g == 2 and o in FINAL_PE:
                        final(t - 1, FINAL_PE[o])
                more = not last_block(n)
                if more:
                    first_codes(n + 1, 1 - par, 0)
                put(n, OCT - 3, False)
                put(n, OCT - 2, False)
                if more:
                    first_codes(n + 1, 1 - par, 1)
                put(n, OCT - 1, False)
                for (u, e, half), spot in zip(units, spots):
                    if spot + DOWN_LAG >= OCT:
                        down(tm, u, e, half)

            pe.wait_ge(b_ones, 4)
            pe.wait_ge(b_codew, 1)
            gate_rest()
            pe.wait_ge(nt_gate_in, 16)
            for g in range(2):
                for pair in range(2):
                    gate(1, g, pair)
            first_codes(0, 0, 0)
            first_codes(0, 0, 1)
            slots(pe, slot)
            turn_x(BPT * TILES, TILES, 3)
            last_units = units_of(BPT - 1)
            for j, unit in enumerate(last_units):
                up(TILES, *unit)
                if j:
                    down(TILES, *last_units[j - 1])
            down(TILES, *last_units[-1])
            for step in range(3):
                final(TILES, step)


def kernel(**inputs):
    import numpy as np
    import concourse.bacc as _bacc
    from concourse import mybir as _mybir
    from concourse.bass_utils import run_bass_kernel_spmd as _run

    g = {k: np.asarray(v) for k, v in inputs.items()}
    f32 = np.float32

    def halves(w, b=None, rows=None):
        a = np.zeros((rows or HALF + (b is not None), 2, w.shape[1]), f32)
        a[0:HALF, 0], a[0:HALF, 1] = w[0:HALF], w[HALF:D]
        if b is not None:
            a[HALF, 1] = b
        return a

    side = SIDE // PATCH
    patches = g["x"].reshape(IMAGES, CHANNELS, side, PATCH, side, PATCH).transpose(0, 1, 3, 5, 2, 4)
    patches = patches.reshape(IMAGES, PCH, 128, PATCHES).transpose(0, 2, 1, 3)
    w_patch = g["L0_tok_proj_w"].T.reshape(PCH, 128, D).transpose(1, 0, 2)

    wqkv, bqkv = g["L0_attn_w_qkv"], g["L0_attn_b_qkv"]
    w_pad = np.zeros((D, 2 * HG, 4, 32), f32)
    b_pad = np.zeros((2 * HG, 4, 32), f32)
    w_pad[..., 0:DH] = wqkv[:, 0:2 * D].reshape(D, 2 * HG, 4, DH)
    b_pad[..., 0:DH] = bqkv[0:2 * D].reshape(2 * HG, 4, DH)
    w_qk = halves(w_pad.reshape(D, -1), b_pad.reshape(-1), 128).reshape(128, 2, 2 * HG, 128)

    p = np.arange(128)
    cols = np.zeros((128, 16), f32)
    for j, name in enumerate(("L0_ffn_m1_b", "L0_ffn_ln_g", "L0_ffn_ln_b")):
        cols[0:HALF, 2 * j:2 * j + 2] = g[name].reshape(2, HALF).T
    cols[:, 8] = -0.5
    cols[:, 12:16] = -1.0
    code = np.zeros((128, 2, 128), f32)
    for a, n in enumerate((HI, LO)):
        for c in range(PER * n):
            at = LOW_P * a + c // n
            code[at, a, c], code[at + PER, a, c], code[LOW_P * a + 2 * PER, a, c] = -1.0, 2.0 * (c % n), 1.0 - (c % n) ** 2
    place = (np.arange(16 + 128)[None, :] == OCT * (p[:, None] // LO) + OCT - 1).astype(f32)
    mask = np.zeros((TOK, 4, TOK), f32)
    mask[np.arange(1, TOK), :, np.arange(1, TOK)] = MASKED
    pos_t = halves(g["L0_ffn_posembed"].T, np.ones(EXPERTS, f32))

    arrays = dict(
        patches=patches, txt=g["txt"], w_patch=w_patch, b_patch=g["L0_tok_proj_b"][None, :], w_qk=w_qk,
        scale=g["L0_attn_scale"], w_v=halves(wqkv[:, 2 * D:], bqkv[2 * D:], 128),
        w_o=halves(g["L0_attn_w_proj"], g["L0_attn_b_proj"], 128),
        pos_t=pos_t, w_pos=halves(g["L0_ffn_pos_w"], g["L0_ffn_pos_b"]), w_gate=halves(g["L0_ffn_gate_w"], g["L0_ffn_gate_b"]),
        b_gate=g["L0_ffn_gate_b"],
        w_shared=halves(np.concatenate([g["L0_ffn_sg_w"], g["L0_ffn_su_w"]], axis=1)).reshape(HALF, 2, 4, D),
        w_sdown=g["L0_ffn_sd_w"].reshape(4, HALF, D).transpose(1, 0, 2),
        w_exp=np.concatenate([g["L0_ffn_eg_w"], g["L0_ffn_eu_w"]], axis=2).transpose(1, 0, 2),
        w_down=g["L0_ffn_ed_w"].reshape(EXPERTS, 2, HALF, D).transpose(2, 0, 1, 3),
        w_m1=halves(g["L0_ffn_m1_w"]), w_m2=halves(g["L0_ffn_m2_w"], g["L0_ffn_m2_b"]), cols=cols,
        ident_in=np.eye(128, dtype=f32), place_in=place, code_in=code, mask_in=mask)

    nc = _bacc.Bacc("TRN2", target_bir_lowering=False, num_devices=1)
    args, maps = {}, {}
    for name, a in arrays.items():
        a = np.ascontiguousarray(a)
        maps[f"in_{name}"] = a
        args[name] = nc.dram_tensor(f"in_{name}", a.shape, _mybir.dt.from_np(a.dtype), kind="ExternalInput").ap()
    out = nc.dram_tensor("out_0", (TOKENS, D), F32, kind="ExternalOutput").ap()
    build(nc, out=out, **args)
    r = _run(nc, [maps], core_ids=[0])
    return r.results[0]["out_0"].reshape(IMAGES, TOK, D)
```
